# Optimizing a Trainium2 kernel written in Bass

```python
import numpy as np
import jax
import jax.numpy as jnp

def _softmax(x, axis=-1):
    return jax.nn.softmax(x, axis=axis)

def _gelu(x):
    return jax.nn.gelu(x, approximate=True)

def _silu(x):
    return jax.nn.silu(x)

def _sigmoid(x):
    return jax.nn.sigmoid(x)

def _layernorm(x, axis=-1, eps=1e-05):
    m = jnp.mean(x, axis=axis, keepdims=True)
    v = jnp.var(x, axis=axis, keepdims=True)
    return (x - m) / jnp.sqrt(v + eps)

def _scatter_add(tgt, idx, src, axis=0):
    return tgt.at[idx].add(src)

def _segment_sum(src, seg, n):
    return jax.ops.segment_sum(src, seg, n)
kernel_name = 'mk_gnn_resnorm_d2_gnn_r32_75f28a'

def setup_inputs(seed: int=0):
    np.random.seed(seed)
    _w = jnp.asarray

    def _rec_inputs():
        import jax
        import jax.numpy as jnp
        _gk = jax.random.key(seed)
        x = -0.0003713 + 1 * jax.random.normal(jax.random.fold_in(_gk, 1), (3125, 128), jnp.float32)
        src = jax.random.randint(jax.random.fold_in(_gk, 2), (100000,), 0, 3125, jnp.int32)
        dst = jax.random.randint(jax.random.fold_in(_gk, 3), (100000,), 0, 3125, jnp.int32)
        _o = jnp.argsort(dst, stable=True)
        src = src[_o]
        dst = dst[_o]
        edge_type_16 = jax.random.randint(jax.random.fold_in(_gk, 12), (100000,), 0, 16, jnp.int32)
        edge_weight = jax.random.uniform(jax.random.fold_in(_gk, 13), (100000,), jnp.float32, 0.0, 0.999998)
        return (x, src, dst, edge_type_16, edge_weight)
    x, src, dst, edge_type_16, edge_weight = _rec_inputs()

    def _L0_gnn_setup():
        import jax, jax.numpy as jnp
        import numpy as np
        LN_EPS = 1e-05
        N_NODES = 3125
        N_EDGES = 50000
        IN_FEATS = 128
        OUT_FEATS = 128
        key = jax.random.key(seed)
        k1, k2, k3, k4, k5 = jax.random.split(key, 5)
        feature = jax.random.normal(k1, (N_NODES, IN_FEATS), dtype=jnp.float32)
        src = jax.random.randint(k2, (N_EDGES,), 0, N_NODES, dtype=jnp.int32)
        dst = jax.random.randint(k3, (N_EDGES,), 0, N_NODES, dtype=jnp.int32)
        W = jax.random.normal(k4, (OUT_FEATS, IN_FEATS), dtype=jnp.float32) * (1.0 / np.sqrt(IN_FEATS))
        b = jax.random.normal(k5, (OUT_FEATS,), dtype=jnp.float32) * 0.01
        gamma = jnp.ones((IN_FEATS,), dtype=jnp.float32)
        beta = jnp.zeros((IN_FEATS,), dtype=jnp.float32)
        return {'feature': feature, 'src': src, 'dst': dst, 'W': W, 'b': b, 'gamma': gamma, 'beta': beta}
    _L0_gnn_all = _L0_gnn_setup()
    _L0_gnn_in = {k: v for k, v in _L0_gnn_all.items() if k in ('W', 'b', 'gamma', 'beta')}
    del _L0_gnn_all

    def _L1_gnn_setup():
        import jax, jax.numpy as jnp
        import numpy as np
        N, E, D, R, H, L = (30000, 15000, 128, 16, 4, 3)
        DH = D // H
        key = jax.random.key(seed)
        ks = jax.random.split(key, 16)
        s = 1.0 / np.sqrt(D)
        return {'feat': jax.random.normal(ks[0], (N, D), jnp.float32), 'src': jax.random.randint(ks[1], (E,), 0, N, jnp.int32), 'dst': jax.random.randint(ks[2], (E,), 0, N, jnp.int32), 'etype': jax.random.randint(ks[3], (E,), 0, R, jnp.int32), 'temporal_weight': jax.random.uniform(ks[4], (E,), jnp.float32), 'W_rel': jax.random.normal(ks[5], (L, R, D, D), jnp.float32) * s, 'b_rel': jnp.zeros((L, D), jnp.float32), 'W_loop': jax.random.normal(ks[6], (L, D, D), jnp.float32) * s, 'W_gat': jax.random.normal(ks[7], (L, D, D), jnp.float32) * s, 'attn_l': jax.random.normal(ks[8], (L, H, DH), jnp.float32) * s, 'attn_r': jax.random.normal(ks[9], (L, H, DH), jnp.float32) * s, 'b_gat': jnp.zeros((L, D), jnp.float32), 'W_fuse': jax.random.normal(ks[10], (2 * D, D), jnp.float32) * (1.0 / np.sqrt(2 * D)), 'b_fuse': jnp.zeros((D,), jnp.float32), 'W_gate': jax.random.normal(ks[11], (D + 1, D), jnp.float32) * s, 'b_gate': jnp.zeros((D,), jnp.float32)}
    _L1_gnn_all = _L1_gnn_setup()
    _L1_gnn_in = {k: v for k, v in _L1_gnn_all.items() if k in ('W_rel', 'b_rel', 'W_loop', 'W_gat', 'attn_l', 'attn_r', 'b_gat', 'W_fuse', 'b_fuse', 'W_gate', 'b_gate')}
    del _L1_gnn_all
    return {'x': x, 'src': src, 'dst': dst, 'edge_type_16': edge_type_16, 'edge_weight': edge_weight, 'L0_gnn_W': _L0_gnn_in['W'], 'L0_gnn_b': _L0_gnn_in['b'], 'L0_gnn_gamma': _L0_gnn_in['gamma'], 'L0_gnn_beta': _L0_gnn_in['beta'], 'L1_gnn_W_rel': _L1_gnn_in['W_rel'], 'L1_gnn_b_rel': _L1_gnn_in['b_rel'], 'L1_gnn_W_loop': _L1_gnn_in['W_loop'], 'L1_gnn_W_gat': _L1_gnn_in['W_gat'], 'L1_gnn_attn_l': _L1_gnn_in['attn_l'], 'L1_gnn_attn_r': _L1_gnn_in['attn_r'], 'L1_gnn_b_gat': _L1_gnn_in['b_gat'], 'L1_gnn_W_fuse': _L1_gnn_in['W_fuse'], 'L1_gnn_b_fuse': _L1_gnn_in['b_fuse'], 'L1_gnn_W_gate': _L1_gnn_in['W_gate'], 'L1_gnn_b_gate': _L1_gnn_in['b_gate']}

def reference(x, src, dst, edge_type_16, edge_weight, L0_gnn_W, L0_gnn_b, L0_gnn_gamma, L0_gnn_beta, L1_gnn_W_rel, L1_gnn_b_rel, L1_gnn_W_loop, L1_gnn_W_gat, L1_gnn_attn_l, L1_gnn_attn_r, L1_gnn_b_gat, L1_gnn_W_fuse, L1_gnn_b_fuse, L1_gnn_W_gate, L1_gnn_b_gate):
    import jax
    import jax.numpy as jnp

    def _L0_gnn_ref(feature, src, dst, W, b, gamma, beta):
        import jax, jax.numpy as jnp
        import numpy as np
        LN_EPS = 1e-05
        N_NODES = 3125
        N_EDGES = 50000
        IN_FEATS = 128
        OUT_FEATS = 128
        n_nodes = feature.shape[0]
        h = jax.ops.segment_sum(feature[src], dst, num_segments=n_nodes)
        mu = jnp.mean(h, axis=-1, keepdims=True)
        var = jnp.var(h, axis=-1, keepdims=True)
        h = (h - mu) * jax.lax.rsqrt(var + LN_EPS) * gamma + beta
        return h @ W.T + b

    def _L1_gnn_ref(feat, src, dst, etype, temporal_weight, W_rel, b_rel, W_loop, W_gat, attn_l, attn_r, b_gat, W_fuse, b_fuse, W_gate, b_gate):
        import jax, jax.numpy as jnp
        import numpy as np
        N, E, D, R, H, L = (30000, 15000, 128, 16, 4, 3)
        DH = D // H
        n = feat.shape[0]
        h = feat
        tw_mean = jnp.mean(temporal_weight)
        for l in range(L):
            ht = jnp.einsum('nd,rdo->nro', h, W_rel[l])
            msg = ht[src, etype]
            h_rel = jax.ops.segment_sum(msg, dst, num_segments=n)
            h_rel = h_rel + h @ W_loop[l] + b_rel[l]
            z = (h @ W_gat[l]).reshape(n, H, DH)
            el = jnp.sum(z * attn_l[l], axis=-1)
            er = jnp.sum(z * attn_r[l], axis=-1)
            e = jax.nn.leaky_relu(el[src] + er[dst], 0.2)
            m = jax.ops.segment_max(e, dst, num_segments=n)
            ex = jnp.exp(e - m[dst])
            denom = jax.ops.segment_sum(ex, dst, num_segments=n)
            alpha = ex / denom[dst]
            h_gat = jax.ops.segment_sum(alpha[:, :, None] * z[src], dst, num_segments=n)
            h_gat = h_gat.reshape(n, D) + b_gat[l]
            hc = jnp.concatenate([h_rel, h_gat], axis=1) @ W_fuse + b_fuse
            if l == 0:
                avg = jnp.full((n, 1), tw_mean, dtype=hc.dtype)
                gate = jax.nn.sigmoid(jnp.concatenate([hc, avg], axis=1) @ W_gate + b_gate)
                hc = hc * gate
            h = jax.nn.relu(hc)
        return h
    x = _layernorm(x + _L0_gnn_ref(x, src, dst, L0_gnn_W, L0_gnn_b, L0_gnn_gamma, L0_gnn_beta), axis=-1)
    x = _layernorm(x + _L1_gnn_ref(x, src, dst, edge_type_16, edge_weight, L1_gnn_W_rel, L1_gnn_b_rel, L1_gnn_W_loop, L1_gnn_W_gat, L1_gnn_attn_l, L1_gnn_attn_r, L1_gnn_b_gat, L1_gnn_W_fuse, L1_gnn_b_fuse, L1_gnn_W_gate, L1_gnn_b_gate), axis=-1)
    return x

_drawn_inputs = setup_inputs


def setup_inputs(seed=0):
    import zlib

    import numpy as np

    out = dict(_drawn_inputs(seed))
    spreads = {'L0_gnn_gamma': (1.0, 0.2),
     'L0_gnn_beta': (0.0, 0.1),
     'L1_gnn_b_rel': (0.0, 0.302),
     'L1_gnn_b_gat': (0.0, 0.295),
     'L1_gnn_b_fuse': (0.0, 0.1),
     'L1_gnn_b_gate': (0.0, 0.399)}
    factors = {'edge_weight': 8.0, 'L0_gnn_b': 3.423, 'L1_gnn_attn_r': 3.077}
    for name, (base, spread) in spreads.items():
        noise = np.random.default_rng([zlib.crc32(name.encode()), seed]).standard_normal(out[name].shape)
        drawn = base * np.exp(spread * noise) if base else spread * noise
        out[name] = jnp.asarray(drawn.astype(out[name].dtype))
    for name, factor in factors.items():
        out[name] = (out[name] * factor).astype(out[name].dtype)
    return out
```

```python
import numpy as np
import concourse.bass as bass
from concourse import mybir
from contextlib import ExitStack

F32 = mybir.dt.float32
I32 = mybir.dt.int32
ALU = mybir.AluOpType
ACT = mybir.ActivationFunctionType
AX = mybir.AxisListType.X

D = 128
N = 3125
E = 100000
R = 16
H = 4
DH = D // H
L = 3
P = 125
TILES = E // P
KT = 5
PASSES = TILES // KT
NP = 5
TS = NP * KT
RING = (0, 1, 2, 0, 1)
SUPERS = PASSES // NP
W = 25
RC = R * W
HC = H * W
CH = 500
CHUNKS = -(-N // CH)
NPAD = CHUNKS * CH
CT = CH // P
ROW = D + H
SR = 80
SC = E // SR
SK = SC // P
WEIGHT_LOADS = 12 + 2 * L
EPS = 1e-5
SLOPE = 0.2


def spread(ap, dim, n):
    ap = ap.unsqueeze(dim)
    shape = list(ap.shape)
    shape[dim] = n
    return ap.broadcast_to(shape)


def build(nc, x, src, dst, etype, eweight, w0, b0, gamma, beta, wrel, brel, wloop, wgat,
          attnl, attnr, bgat, wfuse, bfuse, wgate, bgate, out, tables, x1_dram):
    ctx = ExitStack()
    with ctx:
        def sb(name, shape, dt=F32):
            return ctx.enter_context(nc.sbuf_tensor(name, shape, dt))

        def psum(name, shape):
            return ctx.enter_context(nc.psum_tensor(name, shape, F32))

        def sem(name):
            return ctx.enter_context(nc.semaphore(name))

        ident = sb("ident", [128, 128])
        ones = sb("ones", [128, 128])
        mean_w = sb("mean_w", [128, 128])
        iota = sb("iota", [128, RC])
        pidx_i = sb("pidx_i", [128, 1], I32)
        pidx = sb("pidx", [128, 1])
        eps = sb("eps", [128, 1])
        wrel_sb = sb("wrel_sb", [128, R, D])
        wloop_sb = sb("wloop_sb", [128, L, D])
        wgat_sb = sb("wgat_sb", [128, L, D])
        wfuse_sb = sb("wfuse_sb", [128, 2, D])
        wgate_sb = sb("wgate_sb", [128, D])
        w0t = sb("w0t", [128, D])
        cols = sb("cols", [128, 8 + 2 * L])
        B0, GAMMA, BETA, BFUSE, BGATE, WTW, NGB, TW = range(8)
        BREL, BGAT = 8, 8 + L
        wl = sb("wl", [128, L, H])
        wr = sb("wr", [128, L, H])
        wr_b = sb("wr_b", [128, H, P])
        dst_t = sb("dst_t", [P, TILES])
        ety_t = sb("ety_t", [P, TILES])
        src_t = sb("src_t", [P, TILES], I32)
        gmin0 = sb("gmin0", [P, PASSES])
        gbase = sb("gbase", [P, PASSES])
        gspan = sb("gspan", [P, PASSES])
        base_f = sb("base_f", [P, PASSES])
        base_i = sb("base_i", [P, PASSES], I32)
        rounds_f = sb("rounds_f", [P, 2])
        rounds_i = sb("rounds_i", [P, 1], I32)
        er_b = sb("er_b", [128, H, NPAD])
        acc = sb("acc", [128, 3, NPAD])
        h_t = sb("h_t", [128, NPAD])
        el_all = sb("el_all", [P, CHUNKS * CT, H])
        gmx = sb("gmx", [P, H])
        idx = sb("idx", [P, TS], I32)
        rows = sb("rows", [P, TS, ROW])
        rhs = sb("rhs", [P, 3, KT, RC + HC])
        agg = sb("agg", [128, NP, RC + HC])
        part = sb("part", [128, 3, NP * W])
        ld = sb("ld", [P, TS])
        key_a = sb("key_a", [P, TS])
        key_b = sb("key_b", [P, TS])
        relkey = sb("relkey", [P, TS])
        hit = sb("hit", [P, TS, W])
        att = sb("att", [P, 2, KT, H, W])
        mwin = sb("mwin", [P, 2, H, W])
        tab = sb("tab", [P, CT, ROW])
        small = sb("small", [128, 160])

        agg_flat = agg[:, :, :].rearrange("p a c -> p (a c)")
        hstage = sb("hstage", [128, CH])
        iota_i = agg_flat[:, 0:RC].bitcast(I32)
        stage = [agg_flat[:, i * CH:(i + 1) * CH] for i in range(5)]
        er_flat = er_b[:, :, :].rearrange("p a b -> p (a b)")
        x_t = er_b[:, 0, :]
        seq_i = [er_flat[0:SR, NPAD + i * SC:NPAD + (i + 1) * SC].bitcast(I32) for i in range(3)]
        seq_f = [er_flat[0:SR, NPAD + (3 + i) * SC:NPAD + (4 + i) * SC] for i in range(3)]
        attn_b = [er_flat[:, NPAD + i * 3 * D:NPAD + (i + 1) * 3 * D] for i in range(2)]

        bank = [psum(f"bank{i}", [128, 512]) for i in range(8)]

        s = {}

        def S(name):
            if name not in s:
                s[name] = sem(name)
            return s[name]

        edges_loaded, weights_loaded = S("edges_loaded"), S("weights_loaded")
        wrel_loaded, x_loaded, table_written = S("wrel_loaded"), S("x_loaded"), S("table_written")
        gathered = [sem(f"gathered{i}") for i in range(NP)]

        block = ctx.enter_context(nc.Block())

        seq = lambda a: a.rearrange("(p n) -> p n", p=SR)
        col = lambda a: a.rearrange("(d a) -> d a", a=1)

        @block.sync
        def _(sp):
            for i, a in enumerate((dst, etype, src)):
                sp.dma_start(seq_i[i], seq(a)).then_inc(edges_loaded, 16)
            ld_w = [(w0t[:, :], w0), (wfuse_sb[:, :, :], wfuse.rearrange("(a d) o -> d a o", a=2)),
                    (wgate_sb[:, :], wgate[0:D, :]),
                    (wloop_sb[:, :, :], wloop.rearrange("l d o -> d l o")),
                    (wgat_sb[:, :, :], wgat.rearrange("l d o -> d l o")),
                    (cols[:, WTW:WTW + 1], wgate[D:D + 1, :].rearrange("a d -> d a")),
                    (cols[:, B0:B0 + 1], col(b0)), (cols[:, GAMMA:GAMMA + 1], col(gamma)),
                    (cols[:, BETA:BETA + 1], col(beta)), (cols[:, BFUSE:BFUSE + 1], col(bfuse)),
                    (cols[:, BGATE:BGATE + 1], col(bgate)),
                    (er_flat[0:SR, NPAD + 6 * SC:NPAD + 7 * SC], seq(eweight))]
            for l in range(L):
                ld_w += [(cols[:, BREL + l:BREL + l + 1], col(brel[l])), (cols[:, BGAT + l:BGAT + l + 1], col(bgat[l]))]
            assert len(ld_w) == WEIGHT_LOADS
            for a, b in ld_w:
                sp.dma_start(a, b).then_inc(weights_loaded, 16)
            for n in range(N // P):
                if n >= 2:
                    sp.wait_ge(S("x_transposed"), n - 1)
                sp.dma_start(tab[:, n % 2, 0:D], x[n * P:(n + 1) * P, :]).then_inc(S(f"x_loaded{n % 2}"), 16)
            sp.wait_ge(S("edges_float"), 3)
            for i, a in enumerate((attnl, attnr)):
                sp.dma_start(attn_b[i], a.rearrange("(q l) h j -> q (l h j)", q=1).broadcast_to([128, L * D])
                             ).then_inc(S("attn_loaded"), 16)
            sp.wait_ge(S("x_transposed"), N // P)
            sp.sem_inc(S("tab_free"), 1)
            for l in range(L):
                if l:
                    sp.wait_ge(S("sums_ready"), l + 1)
                sp.dma_start(wrel_sb[:, :, :], wrel[l].rearrange("r d o -> d r o")).then_inc(wrel_loaded, 16)
                for c in range(CHUNKS):
                    sp.wait_ge(S("table_rows"), 2 * (l * CHUNKS + c + 1))
                    sp.dma_start(tables[l][c * CH:(c + 1) * CH, :].rearrange("(k p) f -> p k f", p=P),
                                 tab[:, :, :]).then_inc(table_written, 16)
                    sp.wait_ge(table_written, 16 * (l * CHUNKS + c + 1))
                    sp.sem_inc(S("tab_free"), 1)
                if l == 0:
                    sp.dma_start(x1_dram, h_t[:, :]).then_inc(S("x1_saved"), 16)
            sp.wait_ge(S("x1_saved"), 16)
            sp.wait_ge(S("sums_ready"), L + 1)
            sp.dma_start(er_b[:, 0, :], x1_dram).then_inc(S("x1_back"), 16)
            for c in range(CHUNKS):
                tiles = min(CT, N // P - c * CT)
                sp.wait_ge(S("final_kept"), c + 1)
                sp.dma_start(out[c * CH:c * CH + tiles * P, :].rearrange("(k p) f -> p k f", p=P),
                             tab[:, 0:tiles, 0:D]).then_inc(S("out_written"), 16)
                sp.wait_ge(S("out_written"), 16 * (c + 1))
                sp.sem_inc(S("tab_free"), 1)

        @block.gpsimd
        def _(pool):
            nc.gpsimd.iota(iota_i, [[1, RC]], base=0, channel_multiplier=0).then_inc(S("iotas"), 1)
            nc.gpsimd.iota(pidx_i[:, :], [[0, 1]], base=0, channel_multiplier=1).then_inc(S("iotas"), 1)
            nc.gpsimd.memset(ones[:, :], 1.0).then_inc(S("ones_set"), 1)
            nc.gpsimd.memset(mean_w[:, :], 1.0 / D).then_inc(S("ones_set"), 1)
            nc.gpsimd.memset(eps[:, :], EPS).then_inc(S("passes_done"), NP)
            pool.wait_ge(S("rounds_set"), 1)
            rounds = pool.value_load(rounds_i[0:1, 0:1], min_val=1, max_val=N // W)
            pool.wait_ge(S("edges_tiled"), 6)
            for stage_no in range(L + 1):
                table = x if stage_no == 0 else tables[stage_no - 1]
                width = D if stage_no == 0 else ROW
                if stage_no:
                    pool.wait_ge(table_written, 16 * CHUNKS * stage_no)
                    pool.nop(nofuse=True)
                with pool.Fori(0, rounds) as j:
                    with pool.Fori(0, SUPERS) as sp_no:
                        q = pool.snap((rounds * stage_no + j) * SUPERS + sp_no)
                        for i in range(NP):
                            t0 = i * KT
                            pool.wait_ge(S("passes_done"), q * NP + (i + 1))
                            nc.gpsimd.tensor_copy(idx[:, t0:t0 + KT],
                                                  src_t[:, bass.ds(sp_no * TS + t0, KT)]).then_inc(S("idx_set"), 1)
                            pool.wait_ge(S("idx_set"), q * NP + (i + 1))
                            pool.nop(nofuse=True)
                            for t in range(t0, t0 + KT):
                                pool.indirect_dma_start(
                                    rows[:, t, 0:width], None, table[:, :],
                                    bass.IndirectOffsetOnAxis(ap=idx[:, t:t + 1], axis=0)
                                ).then_inc(gathered[i], 16)

        @block.tensor
        def _(pe):
            def mm(o, a, b, start=True, stop=True):
                return nc.tensor.matmul(o, a, b, start=start, stop=stop)

            pe.wait_ge(S("ident_set"), 1)
            for a in range(3):
                pe.wait_ge(S("edges_float"), a + 1)
                for half in range(2):
                    if a:
                        pe.wait_ge(S("edges_tiled"), 2 * (a - 1) + half + 1)
                    for k in range(5):
                        kk = half * 5 + k
                        t = nc.tensor.transpose(bank[half][0:P, k * SR:(k + 1) * SR],
                                                seq_f[a][:, kk * P:(kk + 1) * P], ident[0:SR, 0:SR])
                    t.then_inc(S("edges_transposed"), 1)
            pe.wait_ge(S("ones_set"), 2)
            pe.wait_ge(S("span_diag"), 4)
            for k in range(4):
                t = mm(bank[2][0:P, k * SR:(k + 1) * SR], ones[0:SR, 0:P],
                       seq_f[2][:, k * SR:(k + 1) * SR])
            t.then_inc(S("spans_spread"), 1)
            pe.wait_ge(weights_loaded, 16 * WEIGHT_LOADS)
            nc.tensor.transpose(bank[3][:, 0:D], w0t[:, :], ident[:, :]).then_inc(S("w0_transposed"), 1)
            pe.wait_ge(S("weight_rows"), 1)
            mm(bank[4][:, 0:1], ones[0:SR, :], small[0:SR, 8:9]).then_inc(S("weight_total"), 1)
            for n in range(N // P):
                pe.wait_ge(S(f"x_loaded{n % 2}"), 16 * (n // 2 + 1))
                if n >= 2:
                    pe.wait_ge(S("x_kept"), n - 1)
                nc.tensor.transpose(bank[5 + n % 2][:, 0:P], tab[:, n % 2, 0:D], ident[0:P, 0:P]
                                    ).then_inc(S("x_transposed"), 1)

            pe.wait_ge(S("rounds_set"), 1)
            rounds = pe.value_load(rounds_i[0:1, 0:1], min_val=1, max_val=N // W)

            def norm(i):
                pe.wait_ge(S("norm_in"), i + 1)
                mm(bank[2][:, 0:CH], mean_w[:, :], stage[0]).then_inc(S("norm_mean"), 1)
                pe.wait_ge(S("norm_square"), i + 1)
                mm(bank[3][:, 0:CH], mean_w[:, :], stage[2]).then_inc(S("norm_var"), 1)

            def new_table(c, l):
                pe.wait_ge(S("h_ready"), c + 1 + l * CHUNKS)
                for k in range(CT):
                    t = nc.tensor.transpose(bank[4][0:P, k * D:(k + 1) * D], hstage[:, k * P:(k + 1) * P], ident[:, :])
                t.then_inc(S("rows_major"), 1)
                for k in range(CT):
                    t = mm(bank[5][0:P, k * H:(k + 1) * H], hstage[:, k * P:(k + 1) * P], wl[:, l, :])
                t.then_inc(S("el_major"), 1)
                for h in range(H):
                    if h >= 2:
                        pe.wait_ge(S("er_kept"), (l * CHUNKS + c) * H + (h - 1))
                    mm(bank[6 + h % 2][0:P, 0:CH], wr_b[:, h, :], hstage[:, :]).then_inc(S("er_major"), 1)
                pe.wait_ge(S("er_kept"), (l * CHUNKS + c + 1) * H)
                pe.wait_ge(S("table_rows"), (l * CHUNKS + c + 1) * 2)
                pe.nop(nofuse=True)

            for stage_no in range(L + 1):
                if stage_no:
                    pe.wait_ge(wrel_loaded, 16 * stage_no)
                    pe.wait_ge(S("el_max"), stage_no)
                    nc.tensor.transpose(bank[5][0:H, 0:P], small[0:P, 0:H], ident[0:P, 0:P]
                                        ).then_inc(S("el_max_t"), 1)
                    pe.wait_ge(S("el_diag"), stage_no)
                    mm(bank[6][0:P, 0:H], ones[0:H, 0:P], small[0:H, 20:20 + H]).then_inc(S("el_max_b"), 1)
                with pe.Fori(0, rounds) as j:
                    with pe.Fori(0, SUPERS) as sp_no:
                        q = pe.snap((rounds * stage_no + j) * SUPERS + sp_no)
                        if stage_no == 0:
                            pe.wait_ge(S("hits_set"), q + 1)
                            pe.wait_ge(S("part_kept"), q + 1)
                            for i in range(NP):
                                pe.wait_ge(gathered[i], (q + 1) * (16 * KT))
                                for t in range(KT):
                                    m = mm(bank[0][:, i * W:(i + 1) * W], rows[:, i * KT + t, 0:D],
                                           hit[:, i * KT + t, :], t == 0, t == KT - 1)
                                m.then_inc(S("passes_done"), 1)
                        else:
                            qa = pe.snap((rounds * (stage_no - 1) + j) * SUPERS + sp_no)
                            for i in range(NP):
                                pe.wait_ge(gathered[i], (q + 1) * (16 * KT))
                                pe.wait_ge(S("onehots"), qa * NP + (i + 1))
                                pe.wait_ge(S("weights_set"), qa * NP + (i + 1))
                                pe.wait_ge(S("agg_kept"), qa * NP + (i + 1))
                                for t in range(KT):
                                    mm(bank[RING[i]][:, 0:RC + HC], rows[:, i * KT + t, 0:D],
                                       rhs[:, RING[i], t, :], t == 0, t == KT - 1)
                                if i == 0:
                                    pe.wait_ge(S("part_kept"), q + 1)
                                for t in range(KT):
                                    m = mm(bank[3][:, i * HC:(i + 1) * HC], ones[0:P, :],
                                           rhs[:, RING[i], t, RC:RC + HC], t == 0, t == KT - 1)
                                m.then_inc(S("passes_done"), 1)
                            pe.wait_ge(S("agg_kept"), qa * NP + (NP + 2))
                            for r in range(R):
                                mm(bank[4][:, 0:NP * W], wrel_sb[:, r, :], agg[:, :, r * W:(r + 1) * W],
                                   r == 0, r == R - 1)
                            for h in range(H):
                                m = mm(bank[5][h * DH:(h + 1) * DH, 0:NP * W],
                                       wgat_sb[:, stage_no - 1, h * DH:(h + 1) * DH],
                                       agg[:, :, RC + h * W:RC + (h + 1) * W])
                            m.then_inc(S("projected"), 1)

                if stage_no == 0:
                    with pe.Fori(0, CHUNKS) as c:
                        norm(c * 2)
                        pe.wait_ge(S("affine"), c + 1)
                        mm(bank[4][:, 0:CH], w0t[:, :], stage[3]).then_inc(S("dense0"), 1)
                        norm(c * 2 + 1)
                        new_table(c, 0)
                else:
                    l = stage_no - 1
                    fb = l * CHUNKS
                    with pe.Fori(0, CHUNKS) as c:
                        pe.wait_ge(S("sums_ready"), stage_no + 1)
                        mm(bank[0][:, 0:CH], wloop_sb[:, l, :], h_t[:, bass.ds(c * CH, CH)]
                           ).then_inc(S("looped"), 1)
                        pe.wait_ge(S("branches"), c + (fb + 1))
                        mm(bank[1][:, 0:CH], wfuse_sb[:, 0, :], stage[0], True, False)
                        mm(bank[1][:, 0:CH], wfuse_sb[:, 1, :], stage[1], False, True).then_inc(S("fused"), 1)
                        if l == 0:
                            pe.wait_ge(S("gate_in"), c + 1)
                            mm(bank[2][:, 0:CH], wgate_sb[:, :], stage[2]).then_inc(S("gated"), 1)
                        if l < L - 1:
                            new_table(c, l + 1)
                        else:
                            norm(c + 2 * CHUNKS)
                            pe.wait_ge(S("final_ready"), c + 1)
                            for k in range(CT):
                                t = nc.tensor.transpose(bank[4][0:P, k * D:(k + 1) * D],
                                                        hstage[:, k * P:(k + 1) * P], ident[:, :])
                            t.then_inc(S("final_major"), 1)
                            pe.wait_ge(S("final_kept"), c + 1)
                            pe.nop(nofuse=True)

        @block.vector
        def _(dve):
            v = nc.vector

            def linker(name, base=0):
                n = [0]

                def link(ins):
                    n[0] += 1
                    ins.then_inc(S(name), 1)
                    dve.wait_ge(S(name), base + n[0])
                return link

            link = linker("dve_prologue")
            dve.wait_ge(S("iotas"), 2)
            v.tensor_copy(iota[:, :], iota_i)
            link(v.tensor_copy(pidx[:, :], pidx_i[:, :]))
            v.memset(part[:, :, :], 0.0)
            dve.wait_ge(S("dve_prologue"), 1)
            link(v.memset(er_b[:, 0, :], 0.0))
            v.tensor_scalar(ident[:, :], iota[:, 0:128], pidx[:, 0:1], None, ALU.is_equal
                            ).then_inc(S("ident_set"), 1)
            link(v.memset(acc[:, :, :], 0.0))
            for a in range(3):
                if a == 0:
                    dve.wait_ge(edges_loaded, 48)
                v.tensor_copy(seq_f[a], seq_i[a]).then_inc(S("edges_float"), 1)
            dve.wait_ge(S("edges_float"), 3)
            two = seq_f[0].rearrange("p (a n) -> p a n", a=2)
            v.tensor_reduce(small[0:SR, 0:2], two, AX, ALU.min)
            link(v.tensor_reduce(small[0:SR, 2:4], two, AX, ALU.max))
            link(v.tensor_tensor(small[0:SR, 4:6], small[0:SR, 2:4], small[0:SR, 0:2], ALU.subtract))
            scale = [1.0, float(W), 1.0]
            dsts = [dst_t, ety_t, src_t]
            for a in range(3):
                for half in range(2):
                    dve.wait_ge(S("edges_transposed"), 2 * a + half + 1)
                    o = dsts[a][:, :].rearrange("p (t k) -> p k t", k=SK)[:, half * 5:(half + 1) * 5, :]
                    i_ = bank[half][0:P, 0:5 * SR].rearrange("p (k t) -> p k t", t=SR)
                    ins = v.tensor_scalar(o, i_, scale[a], None, ALU.mult)
                    ins.then_inc(S("edges_tiled"), 1)
            dve.wait_ge(S("edges_tiled"), 6)
            for k, c in enumerate((0, 1, 4, 5)):
                v.tensor_scalar(seq_f[2][:, k * SR:(k + 1) * SR], ident[0:SR, 0:SR], small[0:SR, c:c + 1], None,
                                ALU.mult).then_inc(S("span_diag"), 1)
            dve.wait_ge(S("spans_spread"), 1)
            for k in range(4):
                o = (gmin0, gspan)[k // 2][:, :].rearrange("p (t a) -> p a t", a=2)[:, k % 2, :]
                ins = v.tensor_copy(o, bank[2][0:P, k * SR:(k + 1) * SR])
            link(ins)
            link(v.tensor_reduce(rounds_f[:, 0:1], gspan[:, :], AX, ALU.max))
            link(v.tensor_scalar(base_f[:, 0:N // W], iota[0:P, 0:N // W], float(W), None, ALU.mult))
            link(v.tensor_scalar(gspan[:, 0:N // W], base_f[:, 0:N // W], rounds_f[:, 0:1], None, ALU.is_le))
            link(v.tensor_reduce(rounds_f[:, 1:2], gspan[:, 0:N // W], AX, ALU.add))
            v.tensor_copy(rounds_i[:, :], rounds_f[:, 1:2]).then_inc(S("rounds_set"), 1)
            dve.wait_ge(weights_loaded, 16 * WEIGHT_LOADS)
            dve.wait_ge(S("w0_transposed"), 1)
            link(v.tensor_copy(w0t[:, :], bank[3][:, 0:D]))
            v.tensor_reduce(small[0:SR, 8:9], er_flat[0:SR, NPAD + 6 * SC:NPAD + 7 * SC], AX, ALU.add
                            ).then_inc(S("weight_rows"), 1)
            dve.wait_ge(S("weight_total"), 1)
            link(v.tensor_scalar(cols[:, TW:TW + 1], bank[4][:, 0:1], -1.0 / E, None, ALU.mult))
            link(v.tensor_scalar(cols[:, NGB:NGB + 1], cols[:, WTW:WTW + 1], cols[:, TW:TW + 1], None, ALU.mult))
            link(v.tensor_tensor(cols[:, NGB:NGB + 1], cols[:, NGB:NGB + 1], cols[:, BGATE:BGATE + 1], ALU.subtract))
            for n in range(N // P):
                dve.wait_ge(S("x_transposed"), n + 1)
                v.tensor_copy(x_t[:, n * P:(n + 1) * P], bank[5 + n % 2][:, 0:P]).then_inc(S("x_kept"), 1)
            dve.wait_ge(S("attn_loaded"), 32)
            for i, o in enumerate((wl, wr)):
                link(v.tensor_tensor(attn_b[i], attn_b[i], wgat_sb[:, :, :].rearrange("p l d -> p (l d)"), ALU.mult))
                ins = v.tensor_reduce(o[:, :, :].rearrange("p l h -> p (l h)"),
                                      attn_b[i].rearrange("p (g j) -> p g j", j=DH), AX, ALU.add)
                link(ins)

            rounds = dve.value_load(rounds_i[0:1, 0:1], min_val=1, max_val=N // W)

            def norm(i):
                dve.wait_ge(S("norm_mean"), i + 1)
                v.tensor_tensor(stage[1], stage[0], bank[2][:, 0:CH], ALU.subtract).then_inc(S("norm_centred"), 1)
                dve.wait_ge(S("norm_deviation"), i + 1)
                v.reciprocal(stage[4], stage[4]).then_inc(S("norm_reciprocal"), 1)
                dve.wait_ge(S("norm_reciprocal"), i + 1)

            def new_table(c, k0):
                v.tensor_copy(h_t[:, bass.ds(c * CH, CH)], hstage[:, :]).then_inc(S("h_ready"), 1)
                dve.wait_ge(S("el_major"), c + (k0 + 1))
                e4 = bank[5][0:P, 0:CT * H].rearrange("p (k h) -> p k h", h=H)
                v.tensor_copy(el_all[:, bass.ds(c * CT, CT), :], e4).then_inc(S("el_kept"), 1)
                dve.wait_ge(S("tab_free"), c + (k0 + 1))
                v.tensor_copy(tab[:, :, D:D + H], e4).then_inc(S("table_rows"), 1)
                dve.wait_ge(S("er_kept"), (c + (k0 + 1)) * H)
                dve.nop(nofuse=True)

            v.memset(small[0:1, 120:121], 0.0).then_inc(S("part_kept"), 1)
            v.memset(small[0:1, 121:122], 0.0).then_inc(S("agg_kept"), 2)
            first_max = True
            for stage_no in range(L + 1):
                l = stage_no - 1
                if stage_no:
                    lk = linker(f"gmax{stage_no}")
                    dve.wait_ge(S("el_kept"), CHUNKS * stage_no)
                    v.tensor_reduce(small[0:P, 0:H], el_all[:, 0:N // P, :].rearrange("p n h -> p h n"), AX, ALU.max
                                    ).then_inc(S("el_max"), 1)
                    v.memset(acc[:, :, :], 0.0)
                    dve.wait_ge(S("el_max_t"), stage_no)
                    lk(v.tensor_reduce(small[0:H, 16:17], bank[5][0:H, 0:P], AX, ALU.max))
                    v.tensor_scalar(small[0:H, 20:20 + H], ident[0:H, 0:H], small[0:H, 16:17], None, ALU.mult
                                    ).then_inc(S("el_diag"), 1)
                    dve.wait_ge(S("el_max_b"), stage_no)
                    lk(v.tensor_copy(gmx[:, :], bank[6][0:P, 0:H]))
                lk = linker(f"round_start{stage_no}")
                lk(v.tensor_copy(gbase[:, :], gmin0[:, :]))
                with dve.Fori(0, rounds) as j:
                    lk = linker(f"round{stage_no}", j * 3)
                    lk(v.tensor_scalar(base_f[:, :], gbase[:, :], float(N), None, ALU.min))
                    lk(v.tensor_copy(base_i[:, :], base_f[:, :]))
                    dve.nop(nofuse=True)
                    with dve.Fori(0, SUPERS) as sp_no:
                        q = dve.snap((rounds * stage_no + j) * SUPERS + sp_no)
                        ql = dve.snap(j * SUPERS + sp_no)
                        bases = [dve.value_load(base_i[0:1, bass.ds(sp_no * NP + i, 1)], min_val=0, max_val=N)
                                 for i in range(NP)]
                        nk = 6 if stage_no else 1
                        lk = linker(f"keys{stage_no}", ql * nk)
                        tb = sp_no * TS
                        b5 = spread(gbase[:, bass.ds(sp_no * NP, NP)], 2, KT)
                        lk(v.tensor_tensor(ld[:, :].rearrange("p (a b) -> p a b", b=KT),
                                           dst_t[:, bass.ds(tb, TS)].rearrange("p (a b) -> p a b", b=KT), b5,
                                           ALU.subtract))
                        if stage_no:
                            lk(v.tensor_scalar(key_a[:, :], ld[:, :], -(W - 1) / 2.0, None, ALU.add))
                            lk(v.tensor_tensor(key_b[:, :], key_a[:, :], key_a[:, :], ALU.mult))
                            lk(v.tensor_scalar(key_a[:, :], key_b[:, :], (W / 2.0) ** 2, 1.0e5, ALU.is_gt, ALU.mult))
                            lk(v.tensor_tensor(key_b[:, :], key_a[:, :], ld[:, :], ALU.add))
                            lk(v.tensor_tensor(relkey[:, :], key_b[:, :], ety_t[:, bass.ds(tb, TS)], ALU.add))
                        if stage_no == 0:
                            dve.wait_ge(S("passes_done"), (q + 1) * NP)
                        v.tensor_tensor(hit[:, :, :], spread(iota[0:P, 0:W], 1, TS),
                                        spread(ld[:, :], 2, W), ALU.is_equal
                                        ).then_inc(S("hits_set"), 1)
                        if stage_no:
                            qa = dve.snap((rounds * l + j) * SUPERS + sp_no)
                            for i in range(NP):
                                b = bases[i]
                                g0 = i * KT
                                lk = linker(f"scores{stage_no}", (ql * NP + i) * 3)
                                er_w = er_b[0:P, :, bass.ds(b, W)]
                                v.tensor_tensor(mwin[:, 0, :, :], er_w, spread(gmx[:, :], 2, W), ALU.add)
                                dve.wait_ge(gathered[i], (q + 1) * (16 * KT))
                                lk(v.tensor_tensor(att[:, 0, :, :, :], spread(er_w, 1, KT),
                                                   spread(rows[:, g0:g0 + KT, D:D + H], 3, W),
                                                   ALU.add))
                                lk(v.scalar_tensor_tensor(out=mwin[:, 1, :, :], in0=mwin[:, 0, :, :], scalar=SLOPE,
                                                          in1=mwin[:, 0, :, :], op0=ALU.mult, op1=ALU.max))
                                lk(v.scalar_tensor_tensor(out=att[:, 1, :, :, :], in0=att[:, 0, :, :, :], scalar=SLOPE,
                                                          in1=att[:, 0, :, :, :], op0=ALU.mult, op1=ALU.max))
                                a1 = att[:, 1, :, :, :].rearrange("p t h w -> p t (h w)")
                                a0 = att[:, 0, :, :, :].rearrange("p t h w -> p t (h w)")
                                v.tensor_tensor(a0, a1, spread(mwin[:, 1, :, :].rearrange("p h w -> p (h w)"), 1, KT), ALU.subtract).then_inc(S("scores_set"), 1)
                                dve.wait_ge(S("passes_done"), q * NP + (i + (NP - 1)))
                                for t in range(KT):
                                    ins = v.tensor_scalar(rhs[:, RING[i], t, 0:RC], iota[0:P, :],
                                                          relkey[:, g0 + t:g0 + t + 1], None, ALU.is_equal)
                                ins.then_inc(S("onehots"), 1)
                                dve.wait_ge(S("exp_taken"), qa * NP + (i + 1))
                                dve.wait_ge(S("hits_set"), q + 1)
                                v.tensor_tensor(
                                    rhs[:, RING[i], :, RC:RC + HC].rearrange("p t (h w) -> p t h w", h=H),
                                    att[:, 1, :, :, :], spread(hit[:, g0:g0 + KT, :], 2, H), ALU.mult
                                ).then_inc(S("weights_set"), 1)
                        dve.wait_ge(S("part_ready"), q + 1)
                        n3 = 3 if stage_no else 1
                        lk = linker(f"added{stage_no}", ql * (NP - 1))
                        for i in range(NP):
                            a = acc[:, 0:n3, bass.ds(bases[i], W)]
                            ins = v.tensor_tensor(a, a, part[:, 0:n3, i * W:(i + 1) * W], ALU.add)
                            if i < NP - 1:
                                lk(ins)
                        ins.then_inc(S("part_kept"), 1)
                    dve.wait_ge(S(f"round{stage_no}"), j * 3 + 2)
                    v.tensor_scalar(gbase[:, :], gbase[:, :], float(W), None, ALU.add
                                    ).then_inc(S(f"round{stage_no}"), 1)
                    dve.wait_ge(S(f"round{stage_no}"), j * 3 + 3)
                    dve.nop(nofuse=True)
                lr = min(stage_no, L - 1)
                v.tensor_copy(wr_b[:, :, :], spread(wr[:, lr, :], 2, P)).then_inc(S("sums_ready"), 1)
                dve.wait_ge(S("sums_ready"), stage_no + 1)

                if stage_no == 0:
                    with dve.Fori(0, CHUNKS) as c:
                        cc = bass.ds(c * CH, CH)
                        v.tensor_copy(stage[0], acc[:, 0, cc]).then_inc(S("norm_in"), 1)
                        norm(c * 2)
                        lk = linker("affine_steps", c)
                        lk(v.tensor_tensor(stage[3], stage[1], stage[4], ALU.mult))
                        v.tensor_scalar(stage[3], stage[3], cols[:, GAMMA:GAMMA + 1], cols[:, BETA:BETA + 1],
                                        ALU.mult, ALU.add).then_inc(S("affine"), 1)
                        dve.wait_ge(S("dense0"), c + 1)
                        v.scalar_tensor_tensor(out=stage[0], in0=bank[4][:, 0:CH], scalar=cols[:, B0:B0 + 1],
                                               in1=x_t[:, cc], op0=ALU.add, op1=ALU.add).then_inc(S("norm_in"), 1)
                        norm(c * 2 + 1)
                        v.tensor_tensor(hstage[:, :], stage[1], stage[4], ALU.mult).then_inc(S("h_stage"), 1)
                        dve.wait_ge(S("h_stage"), c + 1)
                        new_table(c, 0)
                else:
                    fb = l * CHUNKS
                    if l == 0:
                        dve.wait_ge(S("x1_saved"), 16)
                    with dve.Fori(0, CHUNKS) as c:
                        cc = bass.ds(c * CH, CH)
                        lk = linker(f"branch_steps{stage_no}", c * 3)
                        lk(v.tensor_scalar(stage[3], acc[:, 2, cc], 1e-30, None, ALU.max))
                        lk(v.reciprocal(stage[4], stage[3]))
                        lk(v.tensor_tensor(stage[3], acc[:, 1, cc], stage[4], ALU.mult))
                        v.tensor_scalar(stage[1], stage[3], cols[:, BGAT + l:BGAT + l + 1], None, ALU.add)
                        dve.wait_ge(S("looped"), c + (fb + 1))
                        v.scalar_tensor_tensor(out=stage[0], in0=bank[0][:, 0:CH], scalar=cols[:, BREL + l:BREL + l + 1],
                                               in1=acc[:, 0, cc], op0=ALU.add, op1=ALU.add).then_inc(S("branches"), 1)
                        if l == 0:
                            dve.wait_ge(S("gate_exp"), c + 1)
                            lk = linker("gate_steps", c * 2)
                            lk(v.tensor_scalar(stage[3], stage[3], 1.0, None, ALU.add))
                            lk(v.reciprocal(stage[4], stage[3]))
                            v.scalar_tensor_tensor(out=hstage[:, :], in0=stage[2], scalar=0.0, in1=stage[4],
                                                   op0=ALU.max, op1=ALU.mult).then_inc(S("h_stage"), 1)
                            dve.wait_ge(S("h_stage"), c + (CHUNKS + 1))
                        else:
                            dve.wait_ge(S("relu_done"), c + ((l - 1) * CHUNKS + 1))
                        if l < L - 1:
                            new_table(c, (l + 1) * CHUNKS)
                        else:
                            dve.wait_ge(S("x1_back"), 16)
                            v.tensor_tensor(stage[0], hstage[:, :], er_b[:, 0, cc], ALU.add).then_inc(S("norm_in"), 1)
                            norm(c + 2 * CHUNKS)
                            v.tensor_tensor(hstage[:, :], stage[1], stage[4], ALU.mult).then_inc(S("final_ready"), 1)
                            dve.wait_ge(S("final_kept"), c + 1)
                            dve.nop(nofuse=True)

        @block.scalar
        def _(act):
            a_ = nc.scalar
            act.wait_ge(S("rounds_set"), 1)
            rounds = act.value_load(rounds_i[0:1, 0:1], min_val=1, max_val=N // W)
            act.wait_ge(S("passes_done"), NP)

            def norm(i):
                act.wait_ge(S("norm_centred"), i + 1)
                a_.activation(stage[2], stage[1], ACT.Square).then_inc(S("norm_square"), 1)
                act.wait_ge(S("norm_var"), i + 1)
                a_.activation(stage[4], bank[3][:, 0:CH], ACT.Sqrt, bias=eps[:, 0:1]).then_inc(S("norm_deviation"), 1)

            def new_table(c, l):
                k0 = l * CHUNKS
                act.wait_ge(S("rows_major"), c + (k0 + 1))
                act.wait_ge(S("tab_free"), c + (k0 + 1))
                a_.activation(tab[:, :, 0:D], bank[4][0:P, :].rearrange("p (k d) -> p k d", d=D), ACT.Copy
                              ).then_inc(S("table_rows"), 1)
                for h in range(H):
                    act.wait_ge(S("er_major"), (c + k0) * H + (h + 1))
                    a_.activation(er_b[0:P, h, bass.ds(c * CH, CH)], bank[6 + h % 2][0:P, 0:CH], ACT.Copy
                                  ).then_inc(S("er_kept"), 1)

            for stage_no in range(L + 1):
                with act.Fori(0, rounds) as j:
                    with act.Fori(0, SUPERS) as sp_no:
                        q = act.snap((rounds * stage_no + j) * SUPERS + sp_no)
                        if stage_no == 0:
                            act.wait_ge(S("passes_done"), (q + 2) * NP)
                            act.wait_ge(S("part_kept"), q + 1)
                            a_.activation(part[:, 0, :], bank[0][:, 0:NP * W], ACT.Copy).then_inc(S("part_ready"), 1)
                        else:
                            qa = act.snap((rounds * (stage_no - 1) + j) * SUPERS + sp_no)

                            def take_exp(i):
                                act.wait_ge(S("scores_set"), qa * NP + (i + 1))
                                a_.activation(att[:, 1, :, :, :].rearrange("p t h w -> p (t h w)"),
                                              att[:, 0, :, :, :].rearrange("p t h w -> p (t h w)"), ACT.Exp
                                              ).then_inc(S("exp_taken"), 1)

                            def keep_agg(i):
                                act.wait_ge(S("passes_done"), q * NP + (i + (NP + 1)))
                                a_.activation(agg[:, i, :], bank[RING[i]][:, 0:RC + HC], ACT.Copy
                                              ).then_inc(S("agg_kept"), 1)

                            take_exp(0)
                            for i in range(1, NP):
                                take_exp(i)
                                keep_agg(i - 1)
                            keep_agg(NP - 1)
                            act.wait_ge(S("part_kept"), q + 1)
                            for h in range(H):
                                den = bank[3][h * DH:(h + 1) * DH, 0:NP * HC].rearrange("p (i g w) -> p i g w", g=H, w=W)
                                a_.activation(part[h * DH:(h + 1) * DH, 2, :].rearrange("p (i w) -> p i w", w=W),
                                              den[:, :, h, :], ACT.Copy)
                            act.wait_ge(S("projected"), qa + 1)
                            a_.activation(part[:, 0, :], bank[4][:, 0:NP * W], ACT.Copy)
                            a_.activation(part[:, 1, :], bank[5][:, 0:NP * W], ACT.Copy).then_inc(S("part_ready"), 1)

                if stage_no == 0:
                    with act.Fori(0, CHUNKS) as c:
                        norm(c * 2)
                        norm(c * 2 + 1)
                        new_table(c, 0)
                else:
                    l = stage_no - 1
                    fb = l * CHUNKS
                    with act.Fori(0, CHUNKS) as c:
                        act.wait_ge(S("fused"), c + (fb + 1))
                        if l == 0:
                            a_.activation(stage[2], bank[1][:, 0:CH], ACT.Identity, bias=cols[:, BFUSE:BFUSE + 1]
                                          ).then_inc(S("gate_in"), 1)
                            act.wait_ge(S("gated"), c + 1)
                            a_.activation(stage[3], bank[2][:, 0:CH], ACT.Exp, scale=-1.0, bias=cols[:, NGB:NGB + 1]
                                          ).then_inc(S("gate_exp"), 1)
                        else:
                            a_.activation(hstage[:, :], bank[1][:, 0:CH], ACT.Relu, bias=cols[:, BFUSE:BFUSE + 1]
                                          ).then_inc(S("relu_done"), 1)
                        if l < L - 1:
                            new_table(c, l + 1)
                        else:
                            norm(c + 2 * CHUNKS)
                            act.wait_ge(S("final_major"), c + 1)
                            act.wait_ge(S("tab_free"), c + (L * CHUNKS + 1))
                            a_.activation(tab[:, :, 0:D], bank[4][0:P, :].rearrange("p (k d) -> p k d", d=D), ACT.Copy
                                          ).then_inc(S("final_kept"), 1)


NAMES = ["x", "src", "dst", "edge_type_16", "edge_weight", "L0_gnn_W", "L0_gnn_b", "L0_gnn_gamma", "L0_gnn_beta",
         "L1_gnn_W_rel", "L1_gnn_b_rel", "L1_gnn_W_loop", "L1_gnn_W_gat", "L1_gnn_attn_l", "L1_gnn_attn_r",
         "L1_gnn_b_gat", "L1_gnn_W_fuse", "L1_gnn_b_fuse", "L1_gnn_W_gate", "L1_gnn_b_gate"]


def kernel(**inputs):
    import concourse.bacc as bacc
    from concourse.bass_utils import run_bass_kernel_spmd

    nc = bacc.Bacc("TRN2", target_bir_lowering=False, num_devices=1)
    arrays, args = {}, []
    for name in NAMES:
        a = np.ascontiguousarray(inputs[name])
        arrays[f"in_{name}"] = a
        args.append(nc.dram_tensor(f"in_{name}", a.shape, mybir.dt.from_np(a.dtype), kind="ExternalInput").ap())
    out = nc.dram_tensor("out_x", (N, D), F32, kind="ExternalOutput").ap()
    tables = [nc.dram_tensor(f"table{l}", (NPAD, ROW), F32, kind="Internal").ap() for l in range(L)]
    x1_dram = nc.dram_tensor("x1_t", (D, NPAD), F32, kind="Internal").ap()
    build(nc, *args, out, tables, x1_dram)
    return run_bass_kernel_spmd(nc, [arrays], core_ids=[0]).results[0]["out_x"]
```

```python
import numpy as np
import concourse.bass as bass
from concourse import mybir
from contextlib import ExitStack

F32 = mybir.dt.float32
I32 = mybir.dt.int32
BF16 = mybir.dt.bfloat16
F16 = mybir.dt.float16
ALU = mybir.AluOpType
ACT = mybir.ActivationFunctionType
AX = mybir.AxisListType.X

D = 128
N = 3125
E = 100000
R = 16
H = 4
DH = D // H
L = 3
P = 125
TILES = E // P
KT = 4
PASSES = TILES // KT
NP = 5
TS = NP * KT
RING = (0, 1, 2, 0, 1)
SUPERS = PASSES // NP
W = 20
RC = R * W
HC = H * W
CH = 500
CHUNKS = -(-N // CH)
NPAD = CHUNKS * CH
CT = CH // P
CH2 = CT * D
PARTS = 3
SPLIT = D + H
ROW = SPLIT + PARTS * D // 2
SLOTS = TS // CT
SR = 100
SC = E // SR
SK = SC // P
HK = SK // 2
NR = -(-N // W)
FAR = 1.0e30
NONE = -1.0e28
WIDE = 60.0
WEIGHT_LOADS = 13 + 2 * L
EMPTY = 1.0e-37
PAIRS0 = CHUNKS
OUT_PARTS = ((0, 9), (9, 17), (17, N // P))
EPS = 1e-5
SLOPE = 0.2


def spread(ap, dim, n):
    ap = ap.unsqueeze(dim)
    shape = list(ap.shape)
    shape[dim] = n
    return ap.broadcast_to(shape)


def build(nc, x, src, dst, etype, eweight, w0, b0, gamma, beta, wrel, brel, wloop, wgat,
          attnl, attnr, bgat, wfuse, bfuse, wgate, bgate, out, tables, x1_dram, most_dram):
    ctx = ExitStack()
    with ctx:
        def sb(name, shape, dt=F32):
            return ctx.enter_context(nc.sbuf_tensor(name, shape, dt))

        def psum(name, shape):
            return ctx.enter_context(nc.psum_tensor(name, shape, F32))

        def sem(name):
            return ctx.enter_context(nc.semaphore(name))

        ident = sb("ident", [128, 128])
        ones = sb("ones", [128, 128])
        mean_w = sb("mean_w", [128, 128])
        iota = sb("iota", [128, 160])
        pidx_i = sb("pidx_i", [128, 1], I32)
        pidx = sb("pidx", [128, 1])
        eps = sb("eps", [128, 1])
        wrel_sb = sb("wrel_sb", [128, R, D])
        wloop_sb = sb("wloop_sb", [128, L, D])
        wgat_sb = sb("wgat_sb", [128, L, D])
        wfuse_sb = sb("wfuse_sb", [128, 2, D])
        wgate_sb = sb("wgate_sb", [128, D])
        w0t = sb("w0t", [128, D])
        cols = sb("cols", [128, 8 + 2 * L])
        GAMMA, BETA, BFUSE, BGATE, WTW, GB, TW = range(7)
        BREL, BGAT = 8, 8 + L
        centre = sb("centre", [128, 2, D])
        row_w = sb("row_w", [128, SPLIT])
        wl = sb("wl", [128, L, H])
        wr = sb("wr", [128, L, H])
        wr_b = sb("wr_b", [128, H, P])
        dst_t = sb("dst_t", [P, TILES])
        ety_t = sb("ety_t", [P, TILES])
        src_t = sb("src_t", [P, TILES + TS], I32)
        gmin0 = sb("gmin0", [P, PASSES])
        gbase = sb("gbase", [P, PASSES])
        base_i = sb("base_i", [P, SUPERS, 8], I32)
        rounds_f = sb("rounds_f", [P, 2])
        rounds_i = sb("rounds_i", [P, 1], I32)
        er_b = sb("er_b", [128, H, NPAD])
        acc = sb("acc", [128, 3, NPAD])
        h_t = sb("h_t", [128, NPAD])
        el_all = sb("el_all", [P, CHUNKS * CT, H])
        gmx = sb("gmx", [P, H])
        idx = sb("idx", [P, 2, TS], I32)
        rows = sb("rows", [P, TS, ROW])
        var = sb("var", [P, 3, CHUNKS * CT])
        rows_b = rows[:, :, :].bitcast(BF16)
        rel = sb("rel", [P, 3, KT, RC], BF16)
        wts = sb("wts", [P, 3, KT, HC])
        agg_flat = sb("agg_flat", [128, 5 * CH])
        agg = agg_flat[:, 0:NP * (RC + HC)].rearrange("p (a c) -> p a c", a=NP)
        part = sb("part", [128, 3, NP * W])
        ld = sb("ld", [P, TILES])
        iota16 = sb("iota16", [P, RC], F16)
        far = sb("far", [P, TS, W])
        relkey = sb("relkey", [P, TILES])
        att = sb("att", [P, 2, KT, H, W])
        raw, score = att[:, 0, :, :, :], att[:, 1, :, :, :]
        raw_f = raw.rearrange("p t h w -> p t (h w)")
        rest = att[:, :, :, :, :].rearrange("p a t h w -> p (a t h w)")[:, 0:CT * D].rearrange("p (k d) -> p k d", d=D)
        att_flat = att[:, :, :, :, :].rearrange("p a t h w -> p (a t h w)")
        gspan, base_f = att_flat[:, 0:PASSES], att_flat[:, PASSES:2 * PASSES]
        score_f = score.rearrange("p t h w -> p t (h w)")
        mwin = sb("mwin", [P, 2, H, W])
        small = sb("small", [128, 160])
        mwin_f = mwin[:, :, :, :].rearrange("p a h w -> p a (h w)")
        el_wide = small[:, 110:111].bitcast(I32)
        head_of, win_of = small[0:HC, 40:40 + H], small[0:HC, 50:50 + W]
        most_col, most_rhs = small[0:HC, 100:101], small[0:HC, 75:75 + W]
        most_el = acc[0:H, 0, :]

        hstage = sb("hstage", [128, CH])
        iota_i = agg_flat[:, 0:RC].bitcast(I32)
        stage = [agg_flat[:, i * CH:(i + 1) * CH] for i in range(5)]
        er_flat = er_b[:, :, :].rearrange("p a b -> p (a b)")
        tiled = lambda i: er_flat[0:P, i * CHUNKS * CH2:(i + 1) * CHUNKS * CH2]
        x_rows = er_flat[0:P, 0:N // P * D].rearrange("p (k d) -> p k d", d=D)
        normed, squares = tiled(1), tiled(2)
        normed_rows = normed[:, 0:N // P * D].rearrange("p (k d) -> p k d", d=D)
        squares_rows = squares[:, 0:N // P * D].rearrange("p (k d) -> p k d", d=D)
        seq_i = [er_flat[0:SR, NPAD + i * SC:NPAD + (i + 1) * SC].bitcast(I32) for i in range(3)]
        seq_f = [er_flat[0:SR, NPAD + (3 + i) * SC:NPAD + (4 + i) * SC] for i in range(3)]
        attn_b = [er_flat[:, NPAD + i * 3 * D:NPAD + (i + 1) * 3 * D] for i in range(2)]

        banks = psum("banks", [128, 8, 512])
        bank = [banks[:, i, :] for i in range(8)]
        pair = banks[0:P, 4:6, :].rearrange("p b (t c) -> p (b t) c", c=512 // 2)

        s = {}

        def S(name):
            if name not in s:
                s[name] = sem(name)
            return s[name]

        edges_loaded, weights_loaded = S("edges_loaded"), S("weights_loaded")
        wrel_loaded = S("wrel_loaded")
        table_written = [S("table_written0"), S("table_written1")]
        WRITES = (-(-CHUNKS // 2), CHUNKS // 2)
        gathered = [sem(f"gathered{i}") for i in range(NP)]
        gather_sems = range(gathered[0].num, gathered[0].num + NP)
        assert [g.num for g in gathered] == list(gather_sems)

        block = ctx.enter_context(nc.Block())

        seq = lambda a: a.rearrange("(p n) -> p n", p=SR)
        col = lambda a: a.rearrange("(d a) -> d a", a=1)

        @block.sync
        def _(sp):
            for i, a in enumerate((dst, etype, src)):
                sp.dma_start(seq_i[i], seq(a)).then_inc(edges_loaded, 16)
            ld_w = [(w0t[:, :], w0), (wfuse_sb[:, :, :], wfuse.rearrange("(a d) o -> d a o", a=2)),
                    (wgate_sb[:, :], wgate[0:D, :]),
                    (wloop_sb[:, :, :], wloop.rearrange("l d o -> d l o")),
                    (wgat_sb[:, :, :], wgat.rearrange("l d o -> d l o")),
                    (cols[:, WTW:WTW + 1], wgate[D:D + 1, :].rearrange("a d -> d a")),
                    (cols[:, GAMMA:GAMMA + 1], col(gamma)),
                    (cols[:, BETA:BETA + 1], col(beta)), (cols[:, BFUSE:BFUSE + 1], col(bfuse)),
                    (cols[:, BGATE:BGATE + 1], col(bgate)),
                    (er_flat[0:SR, NPAD + 6 * SC:NPAD + 7 * SC], seq(eweight)),
                    (x_rows, x.rearrange("(k p) d -> p k d", p=P)),
                    (stage[3][0:P, 0:D], b0.rearrange("(q d) -> q d", q=1).broadcast_to([P, D]))]
            for l in range(L):
                ld_w += [(cols[:, BREL + l:BREL + l + 1], col(brel[l])), (cols[:, BGAT + l:BGAT + l + 1], col(bgat[l]))]
            assert len(ld_w) == WEIGHT_LOADS
            for a, b in ld_w:
                sp.dma_start(a, b).then_inc(weights_loaded, 16)
            sp.wait_ge(S("edges_float"), 3)
            for i, a in enumerate((attnl, attnr)):
                sp.dma_start(attn_b[i], a.rearrange("(q l) h j -> q (l h j)", q=1).broadcast_to([128, L * D])
                             ).then_inc(S("attn_loaded"), 16)
            sp.wait_ge(S("rounds_set"), 1)
            rounds = sp.value_load(rounds_i[0:1, 0:1], min_val=1, max_val=NR)
            wide = sp.alloc_register("wide")
            sp_bases = [sp.alloc_register(f"window{i}") for i in range(NP)]
            for l in range(L):
                if l:
                    sp.wait_ge(S("sums_ready"), l + 1)
                sp.dma_start(wrel_sb[:, :, :], wrel[l].rearrange("r d o -> d r o")).then_inc(wrel_loaded, 16)
                if l == 0:
                    sp.wait_ge(S("h_set"), CHUNKS)
                    sp.dma_start(x1_dram, h_t[:, :]).then_inc(S("x1_saved"), 16)
                for c in range(CHUNKS):
                    sp.wait_ge(S("table_rows"), l * CHUNKS + c + 1)
                    if c >= 2:
                        sp.wait_ge(table_written[c % 2], 16 * (l * WRITES[c % 2] + c // 2))
                    sp.dma_start(tables[l][c * CH:(c + 1) * CH, :].rearrange("(k p) f -> p k f", p=P),
                                 rows[:, c % SLOTS * CT:(c % SLOTS + 1) * CT, :]).then_inc(table_written[c % 2], 16)
                sp.wait_ge(S("el_wide_set"), l + 1)
                sp.nop(nofuse=True)
                sp.load(wide, el_wide[0:1, :])
                with sp.If_eq(wide, 1):
                    sp.wait_ge(S(f"most_ready{l}"), 1)
                    sp.dma_start(most_dram, most_el).then_inc(S(f"most_saved{l}"), 16)
                    sp.wait_ge(S(f"most_saved{l}"), 16)
                    sp.nop(nofuse=True)
                    with sp.Fori(0, rounds) as j:
                        sp.wait_ge(S(f"bases_set{l}"), j + 1)
                        sp.nop(nofuse=True)
                        with sp.Fori(0, SUPERS) as sp_no:
                            sp.load(sp_bases, base_i[0:1, bass.ds(sp_no, 1), 0:NP])
                            for i in range(NP):
                                at = sp.snap(sp_bases[i], min_val=0, max_val=N)
                                sp.wait_ge(S(f"window_used{l}"), (j * SUPERS + sp_no) * NP + (i + 1))
                                sp.nop(nofuse=True)
                                sp.dma_start(mwin[:, 0, :, :],
                                             most_dram[:, bass.ds(at, W)].unsqueeze(0).broadcast_to([P, H, W])
                                             ).then_inc(S(f"window_loaded{l}"), 16)
            sp.wait_ge(S("x1_saved"), 16)
            sp.wait_ge(S("sums_ready"), L + 1)
            sp.dma_start(er_b[:, 0, :], x1_dram).then_inc(S("x1_back"), 16)
            for n, (a, b) in enumerate(OUT_PARTS):
                sp.wait_ge(S("out_rows"), n + 1)
                sp.dma_start(out[a * P:b * P, :].rearrange("(k p) f -> p k f", p=P),
                             normed_rows[:, a:b, :]).then_inc(S("out_written"), 16)
            sp.wait_ge(S("out_written"), 16 * len(OUT_PARTS))

        @block.gpsimd
        def _(pool):
            nc.gpsimd.iota(iota_i, [[1, RC]], base=0, channel_multiplier=0).then_inc(S("iotas"), 1)
            nc.gpsimd.iota(pidx_i[:, :], [[0, 1]], base=0, channel_multiplier=1).then_inc(S("iotas"), 1)
            nc.gpsimd.memset(ones[:, :], 1.0).then_inc(S("ones_set"), 1)
            nc.gpsimd.memset(mean_w[:, :], 1.0 / D).then_inc(S("ones_set"), 1)
            nc.gpsimd.memset(eps[:, :], EPS).then_inc(S("passes_done"), NP)
            nc.gpsimd.memset(small[0:1, 140:141], 0.0).then_inc(S("rows_major"), 1)
            pool.wait_ge(S("rounds_set"), 1)
            wide = pool.alloc_register("wide")
            rounds = pool.value_load(rounds_i[0:1, 0:1], min_val=1, max_val=NR)
            pool.wait_ge(S("edges_tiled"), 6)
            nc.gpsimd.tensor_copy(src_t[:, TILES:TILES + TS], src_t[:, 0:TS]).then_inc(S("src_wrapped"), 1)
            nc.gpsimd.tensor_copy(idx[:, 0, :], src_t[:, 0:TS]).then_inc(S("idx_set"), 1)
            pool.wait_ge(S("src_wrapped"), 1)

            pool.sem_inc(S("restarted"), 1)

            def restart(done):
                pool.nop(nofuse=True)
                pool.dma_reset(gather_sems)
                pool.sem_clear(gather_sems)
                pool.sem_inc(S(done), 1)

            for stage_no in range(L + 1):
                l = stage_no - 1
                table = x if stage_no == 0 else tables[l]
                width = D if stage_no == 0 else ROW
                if stage_no:
                    for k in range(2):
                        pool.wait_ge(table_written[k], 16 * WRITES[k] * stage_no)
                    pool.wait_ge(S("el_wide_set"), stage_no)
                    pool.nop(nofuse=True)
                    pool.load(wide, el_wide[0:1, :])
                    with pool.If_eq(wide, 1):
                        pool.sem_inc(S(f"most_restarted{l}"), 1)
                        with pool.Fori(0, rounds) as j:
                            with pool.Fori(0, PASSES) as g:
                                pool.wait_ge(S(f"most_cols{l}"), j * PASSES + (g + 1))
                                nc.gpsimd.tensor_copy(idx[:, 0, 0:KT], src_t[:, bass.ds(g * KT, KT)]
                                                      ).then_inc(S(f"most_idx{l}"), 1)
                                pool.wait_ge(S(f"most_idx{l}"), j * PASSES + (g + 1))
                                pool.nop(nofuse=True)
                                for t in range(KT):
                                    pool.indirect_dma_start(
                                        rows[:, t, 0:width], None, table[:, :],
                                        bass.IndirectOffsetOnAxis(ap=idx[:, 0, t:t + 1], axis=0)
                                    ).then_inc(gathered[0], 16)
                            pool.wait_ge(S(f"most_cols{l}"), (j + 1) * PASSES + 1)
                            restart(f"most_restarted{l}")
                        nc.gpsimd.tensor_copy(idx[:, 0, :], src_t[:, 0:TS]).then_inc(S(f"most_idx{l}"), 1)
                        pool.wait_ge(S(f"most_idx{l}"), rounds * PASSES + 1)
                        pool.nop(nofuse=True)
                with pool.Fori(0, rounds) as j:
                    with pool.Fori(0, SUPERS // 2) as two:
                        for b in range(2):
                            sp_no = pool.snap(two * 2 + b)
                            q = pool.snap((rounds * stage_no + j) * SUPERS + sp_no)
                            pool.wait_ge(S("idx_set"), q + 1)
                            for i in range(NP):
                                pool.wait_ge(S("passes_done"), q * NP + (i + 1))
                                pool.nop(nofuse=True)
                                if i == NP - 1:
                                    nc.gpsimd.tensor_copy(idx[:, 1 - b, :], src_t[:, bass.ds((sp_no + 1) * TS, TS)]
                                                          ).then_inc(S("idx_set"), 1)
                                for t in range(i * KT, (i + 1) * KT):
                                    pool.indirect_dma_start(
                                        rows[:, t, 0:width], None, table[:, :],
                                        bass.IndirectOffsetOnAxis(ap=idx[:, b, t:t + 1], axis=0)
                                    ).then_inc(gathered[i], 16)
                    pool.wait_ge(S("passes_done"), ((rounds * stage_no + j) * SUPERS + (SUPERS + 1)) * NP)
                    if stage_no:
                        pool.wait_ge(S("scores_set"), ((rounds * l + j) * SUPERS + SUPERS) * NP)
                    restart("restarted")

                if stage_no == L:
                    pool.wait_ge(S("x1_back"), 16)
                if stage_no:
                    pool.wait_ge(S("h_set"), stage_no * CHUNKS + 1)
                    pool.nop(nofuse=True)
                with pool.Fori(0, CHUNKS) as c:
                    cc = bass.ds(c * CH, CH)
                    n = pool.snap(stage_no * CHUNKS + c)
                    pool.wait_ge(S("h_set"), n + 1)
                    pool.wait_ge(S("rows_major"), n + 1)
                    pool.nop(nofuse=True)
                    if stage_no == 1:
                        nc.gpsimd.tensor_tensor(hstage[:, :], h_t[:, cc], acc[:, 2, cc], ALU.mult
                                                ).then_inc(S("h_staged"), 1)
                        pool.wait_ge(S("h_staged"), n + 1)
                        pool.nop(nofuse=True)
                        nc.gpsimd.tensor_copy(h_t[:, cc], hstage[:, :]).then_inc(S("h_gated"), 1)
                        pool.wait_ge(S("h_gated"), c + 1)
                        pool.nop(nofuse=True)
                    elif stage_no == L:
                        nc.gpsimd.tensor_tensor(hstage[:, :], h_t[:, cc], er_b[:, 0, cc], ALU.add
                                                ).then_inc(S("h_staged"), 1)
                    else:
                        nc.gpsimd.tensor_copy(hstage[:, :], h_t[:, cc]).then_inc(S("h_staged"), 1)

        @block.tensor
        def _(pe):
            def mm(o, a, b, start=True, stop=True):
                return nc.tensor.matmul(o, a, b, start=start, stop=stop)

            pe.wait_ge(S("ident_set"), 1)
            for a in range(3):
                pe.wait_ge(S("edges_float"), a + 1)
                for half in range(2):
                    if a:
                        pe.wait_ge(S("edges_tiled"), 2 * (a - 1) + half + 1)
                    for k in range(HK):
                        kk = half * HK + k
                        t = nc.tensor.transpose(bank[half][0:P, k * SR:(k + 1) * SR],
                                                seq_f[a][:, kk * P:(kk + 1) * P], ident[0:SR, 0:SR])
                    t.then_inc(S("edges_transposed"), 1)
            pe.wait_ge(S("ones_set"), 2)
            pe.wait_ge(S("span_diag"), 4)
            for k in range(4):
                t = mm(bank[2][0:P, k * SR:(k + 1) * SR], ones[0:SR, 0:P],
                       seq_f[2][:, k * SR:(k + 1) * SR])
            t.then_inc(S("spans_spread"), 1)
            pe.wait_ge(weights_loaded, 16 * WEIGHT_LOADS)
            nc.tensor.transpose(bank[3][:, 0:D], w0t[:, :], ident[:, :]).then_inc(S("w0_transposed"), 1)
            for l in range(L):
                t = nc.tensor.transpose(bank[5][:, l * D:(l + 1) * D], wloop_sb[:, l, :], ident[:, :])
            t.then_inc(S("loops_transposed"), 1)
            mm(bank[6][:, 0:L], wfuse_sb[:, 0, :], cols[:, BREL:BREL + L], True, False)
            mm(bank[6][:, 0:L], wfuse_sb[:, 1, :], cols[:, BGAT:BGAT + L], False, True).then_inc(S("biases_fused"), 1)
            pe.wait_ge(S("w0_scaled"), 1)
            mm(bank[3][:, D:2 * D], centre[:, 0, :], w0t[:, :]).then_inc(S("w0_folded"), 1)
            mm(bank[7][0:P, 0:D], stage[3][:, D:D + P], stage[4][:, 0:D]).then_inc(S("beta_row"), 1)
            pe.wait_ge(S("loops_kept"), 1)
            for l in range(L):
                m = mm(bank[0][:, l * D:(l + 1) * D], stage[2][:, l * D:(l + 1) * D], wfuse_sb[:, 0, :])
            m.then_inc(S("loops_fused"), 1)
            pe.wait_ge(S("weight_rows"), 1)
            mm(bank[4][:, 0:1], ones[0:SR, :], small[0:SR, 8:9]).then_inc(S("weight_total"), 1)
            pe.wait_ge(S("rounds_set"), 1)
            wide = pe.alloc_register("wide")
            rounds = pe.value_load(rounds_i[0:1, 0:1], min_val=1, max_val=NR)

            def rows_product(n, width, w):
                pe.wait_ge(S("h_staged"), n + 1)
                pe.wait_ge(S("pair_kept"), PAIRS0 + n + 1)
                for k in range(CT):
                    t = mm(pair[:, k, 0:width], hstage[:, k * P:(k + 1) * P], w)
                t.then_inc(S("rows_major"), 1)

            def project(stage_no, qa):
                pe.wait_ge(S("agg_kept"), qa * NP + 2 * stage_no)
                pe.wait_ge(S("part_ready"), qa + stage_no)
                for r in range(R):
                    mm(bank[4][:, 0:NP * W], wrel_sb[:, r, :], agg[:, :, r * W:(r + 1) * W],
                       r == 0, r == R - 1)
                for h in range(H):
                    m = mm(bank[5][h * DH:(h + 1) * DH, 0:NP * W],
                           wgat_sb[:, stage_no - 1, h * DH:(h + 1) * DH],
                           agg[:, :, RC + h * W:RC + (h + 1) * W])
                m.then_inc(S("projected"), 1)

            for stage_no in range(L + 1):
                if stage_no:
                    pe.wait_ge(wrel_loaded, 16 * stage_no)
                    pe.wait_ge(S("el_max"), stage_no)
                    nc.tensor.transpose(bank[5][0:2 * H, 0:P], small[0:P, 0:2 * H], ident[0:P, 0:P]
                                        ).then_inc(S("el_max_t"), 1)
                    pe.wait_ge(S("el_diag"), stage_no)
                    mm(bank[6][0:P, 0:2 * H], ones[0:2 * H, 0:P], small[0:2 * H, 20:20 + 2 * H]
                       ).then_inc(S("el_max_b"), 1)
                    pe.wait_ge(S("el_wide_set"), stage_no)
                    pe.nop(nofuse=True)
                    pe.load(wide, el_wide[0:1, :])
                    l = stage_no - 1
                    with pe.If_eq(wide, 1):
                        with pe.Fori(0, rounds) as j:
                            with pe.Fori(0, PASSES) as g:
                                pe.wait_ge(S(f"most_cols{l}"), j * PASSES + (g + 2))
                                nc.tensor.transpose(bank[7][0:HC, 0:P], mwin_f[:, 0, :], ident[0:P, 0:P]
                                                    ).then_inc(S(f"most_turned{l}"), 1)
                                pe.wait_ge(S(f"most_spread{l}"), j * PASSES + (g + 1))
                                mm(bank[6][0:H, 0:W], head_of, most_rhs).then_inc(S(f"most_heads{l}"), 1)
                        pe.wait_ge(S(f"most_restarted{l}"), rounds + 1)
                        pe.nop(nofuse=True)
                    if stage_no >= 2:
                        pe.wait_ge(S("h_gated"), CHUNKS)
                    with pe.Fori(0, CHUNKS) as c:
                        for h in range(H):
                            n = pe.snap((c + l * CHUNKS) * H + h)
                            pe.wait_ge(S("er_kept"), n + 1)
                            mm(bank[6 + h % 2][0:P, 0:CH], wr_b[:, h, :], h_t[:, bass.ds(c * CH, CH)]
                               ).then_inc(S("er_major"), 1)
                    pe.wait_ge(S("zeros_set"), stage_no)
                    for k in (RING[3], RING[4], 3):
                        m = mm(bank[k][:, 0:RC + HC], ones[:, :], agg_flat[:, 0:RC + HC])
                    m.then_inc(S("banks_zeroed"), 1)
                with pe.Fori(0, rounds) as j:
                    pe.wait_ge(S("restarted"), j + (1 if stage_no == 0 else rounds * stage_no + 1))
                    pe.nop(nofuse=True)
                    with pe.Fori(0, SUPERS) as sp_no:
                        q = pe.snap((rounds * stage_no + j) * SUPERS + sp_no)
                        if stage_no == 0:
                            pe.wait_ge(S("hits_set"), q + 1)
                            pe.wait_ge(S("sum_kept"), q + 1)
                            for i in range(NP):
                                pe.wait_ge(gathered[i], (sp_no + 1) * (16 * KT))
                                for t in range(KT):
                                    m = mm(bank[0][:, i * W:(i + 1) * W], rows[:, i * KT + t, 0:D],
                                           far[:, i * KT + t, :], t == 0, t == KT - 1)
                                m.then_inc(S("passes_done"), 1)
                        else:
                            qa = pe.snap((rounds * (stage_no - 1) + j) * SUPERS + sp_no)
                            for i in range(NP):
                                pe.wait_ge(gathered[i], (sp_no + 1) * (16 * KT))
                                pe.wait_ge(S("onehots"), qa * NP + (i + 1))
                                pe.wait_ge(S("agg_kept"), qa * NP + (2 * (stage_no - 1) + (1, 2, 2, 3, 4)[i]))
                                for t in range(KT):
                                    for k in range(PARTS):
                                        c0 = 2 * SPLIT + k * D
                                        mm(bank[RING[i]][:, 0:RC], rows_b[:, i * KT + t, c0:c0 + D],
                                           rel[:, RING[i], t, :], t == 0 and k == 0, t == KT - 1 and k == PARTS - 1)
                                pe.wait_ge(S("weights_set"), qa * NP + (i + 2))
                                for t in range(KT):
                                    mm(bank[RING[i]][:, RC:RC + HC], rows[:, i * KT + t, 0:D],
                                       wts[:, RING[i], t, :], t == 0, t == KT - 1)
                                if i == 0:
                                    pe.wait_ge(S("den_kept"), qa + stage_no)
                                for t in range(KT):
                                    m = mm(bank[3][:, i * HC:(i + 1) * HC], ones[0:P, :],
                                           wts[:, RING[i], t, :], t == 0, t == KT - 1)
                                m.then_inc(S("passes_done"), 1)
                                if i == 0:
                                    project(stage_no, qa)
                if stage_no:
                    project(stage_no, pe.snap(rounds * (SUPERS * stage_no)))

                if stage_no == 0:
                    with pe.Fori(0, CHUNKS) as c:
                        pe.wait_ge(S("sums_staged"), c + 1)
                        for k in range(CT):
                            t = mm(pair[:, k, :], hstage[:, k * P:(k + 1) * P],
                                   centre[:, :, :].rearrange("p a d -> p (a d)"))
                        t.then_inc(S("sums_centred"), 1)
                    pe.wait_ge(S("x1_rows"), 1)
                    for c in range(CHUNKS):
                        if c >= 2:
                            pe.wait_ge(S("h_set"), c - 1)
                        for k in range(c * CT, min((c + 1) * CT, N // P)):
                            t = nc.tensor.transpose(bank[c % 2][:, (k - c * CT) * P:(k - c * CT + 1) * P],
                                                    normed_rows[:, k, :], ident[0:P, 0:P])
                        t.then_inc(S("x1_turned"), 1)
                else:
                    l = stage_no - 1
                    pe.wait_ge(S("sums_ready"), stage_no + 1)
                    pe.nop(nofuse=True)
                    with pe.Fori(0, CHUNKS) as c:
                        n = pe.snap(c + l * CHUNKS)
                        cc = bass.ds(c * CH, CH)
                        pe.wait_ge(S("h_set"), n + CHUNKS)
                        mm(bank[1][:, 0:CH], wfuse_sb[:, 0, :], acc[:, 0, cc], True, False)
                        mm(bank[1][:, 0:CH], wloop_sb[:, l, :], h_t[:, cc], False, False)
                        pe.wait_ge(S("branches"), n + 1)
                        mm(bank[1][:, 0:CH], wfuse_sb[:, 1, :], acc[:, 1, cc], False, True).then_inc(S("fused"), 1)
                        if l == 0:
                            pe.wait_ge(S("gate_in"), c + 1)
                            mm(bank[2][:, 0:CH], wgate_sb[:, :], acc[:, 0, cc]).then_inc(S("gated"), 1)
                with pe.Fori(0, CHUNKS) as c:
                    n = pe.snap(c + stage_no * CHUNKS)
                    if stage_no < L:
                        rows_product(n, SPLIT, row_w[:, :])
                    else:
                        rows_product(n, D, centre[:, 0, :])

        @block.vector
        def _(dve):
            v = nc.vector

            def linker(name, base=0):
                n = [0]

                def link(ins):
                    n[0] += 1
                    ins.then_inc(S(name), 1)
                    dve.wait_ge(S(name), base + n[0])
                return link

            link = linker("dve_prologue")
            dve.wait_ge(S("iotas"), 2)
            v.tensor_copy(iota[:, :], iota_i[:, 0:160])
            v.tensor_copy(iota16[:, :], iota_i[0:P, :])
            link(v.tensor_copy(pidx[:, :], pidx_i[:, :]))
            v.memset(part[:, :, :], 0.0)
            dve.wait_ge(S("dve_prologue"), 1)
            link(v.memset(h_t[:, :], 0.0))
            v.tensor_scalar(ident[:, :], iota[:, 0:128], pidx[:, 0:1], None, ALU.is_equal
                            ).then_inc(S("ident_set"), 1)
            link(v.memset(acc[:, :, :], 0.0))
            for a in range(3):
                if a == 0:
                    dve.wait_ge(edges_loaded, 48)
                v.tensor_copy(seq_f[a], seq_i[a]).then_inc(S("edges_float"), 1)
            dve.wait_ge(S("edges_float"), 3)
            two = seq_f[0].rearrange("p (a n) -> p a n", a=2)
            v.tensor_reduce(small[0:SR, 0:2], two, AX, ALU.min)
            link(v.tensor_reduce(small[0:SR, 2:4], two, AX, ALU.max))
            link(v.tensor_tensor(small[0:SR, 4:6], small[0:SR, 2:4], small[0:SR, 0:2], ALU.subtract))
            scale = [1.0, float(W), 1.0]
            dsts = [dst_t, ety_t, src_t]
            for a in range(3):
                for half in range(2):
                    dve.wait_ge(S("edges_transposed"), 2 * a + half + 1)
                    o = dsts[a][:, 0:TILES].rearrange("p (t k) -> p k t", k=SK)[:, half * HK:(half + 1) * HK, :]
                    i_ = bank[half][0:P, 0:HK * SR].rearrange("p (k t) -> p k t", t=SR)
                    ins = v.tensor_scalar(o, i_, scale[a], None, ALU.mult)
                    ins.then_inc(S("edges_tiled"), 1)
            dve.wait_ge(S("edges_tiled"), 6)
            for k, c in enumerate((0, 1, 4, 5)):
                v.tensor_scalar(seq_f[2][:, k * SR:(k + 1) * SR], ident[0:SR, 0:SR], small[0:SR, c:c + 1], None,
                                ALU.mult).then_inc(S("span_diag"), 1)
            dve.wait_ge(S("spans_spread"), 1)
            for k in range(4):
                o = (gmin0[:, :], gspan)[k // 2].rearrange("p (t a) -> p a t", a=2)[:, k % 2, :]
                ins = v.tensor_copy(o, bank[2][0:P, k * SR:(k + 1) * SR])
            link(ins)
            link(v.tensor_reduce(rounds_f[:, 0:1], gspan, AX, ALU.max))
            link(v.tensor_scalar(base_f[:, 0:NR], iota[0:P, 0:NR], float(W), None, ALU.mult))
            link(v.tensor_scalar(gspan[:, 0:NR], base_f[:, 0:NR], rounds_f[:, 0:1], None, ALU.is_le))
            link(v.tensor_reduce(rounds_f[:, 1:2], gspan[:, 0:NR], AX, ALU.add))
            v.tensor_copy(rounds_i[:, :], rounds_f[:, 1:2]).then_inc(S("rounds_set"), 1)
            dve.wait_ge(weights_loaded, 16 * WEIGHT_LOADS)
            dve.wait_ge(S("w0_transposed"), 1)
            v.tensor_scalar(w0t[:, :], bank[3][:, 0:D], cols[:, GAMMA:GAMMA + 1], None, ALU.mult)
            v.tensor_copy(stage[4][:, 0:D], bank[3][:, 0:D])
            v.tensor_scalar(stage[3][:, D:D + P], mean_w[:, 0:P], float(D), cols[:, BETA:BETA + 1], ALU.mult, ALU.mult)
            v.tensor_tensor(centre[:, 0, :], ident[:, :], mean_w[:, :], ALU.subtract)
            v.tensor_copy(row_w[:, 0:D], ident[:, :]).then_inc(S("w0_scaled"), 1)
            dve.wait_ge(S("loops_transposed"), 1)
            v.tensor_copy(stage[2][:, 0:L * D], bank[5][:, 0:L * D]).then_inc(S("loops_kept"), 1)
            v.tensor_reduce(small[0:SR, 8:9], er_flat[0:SR, NPAD + 6 * SC:NPAD + 7 * SC], AX, ALU.add
                            ).then_inc(S("weight_rows"), 1)
            dve.wait_ge(S("weight_total"), 1)
            link(v.tensor_scalar(cols[:, TW:TW + 1], bank[4][:, 0:1], 1.0 / E, None, ALU.mult))
            link(v.tensor_scalar(cols[:, GB:GB + 1], cols[:, WTW:WTW + 1], cols[:, TW:TW + 1],
                                 cols[:, BGATE:BGATE + 1], ALU.mult, ALU.add))
            dve.wait_ge(S("biases_fused"), 1)
            v.tensor_scalar(cols[:, BREL:BREL + L], bank[6][:, 0:L], cols[:, BFUSE:BFUSE + 1], None, ALU.add)
            dve.wait_ge(S("w0_folded"), 1)
            v.tensor_copy(centre[:, 1, :], bank[3][:, D:2 * D])
            dve.wait_ge(S("beta_row"), 1)
            link(v.tensor_tensor(stage[3][0:P, 0:D], stage[3][0:P, 0:D], bank[7][0:P, 0:D], ALU.add))
            v.tensor_tensor(x_rows, x_rows, spread(stage[3][0:P, 0:D], 1, N // P), ALU.add)
            dve.wait_ge(S("loops_fused"), 1)
            v.tensor_copy(wloop_sb[:, :, :].rearrange("p l d -> p (l d)"), bank[0][:, 0:L * D]
                          ).then_inc(S("folded"), 1)
            dve.wait_ge(S("attn_loaded"), 32)
            for i, o in enumerate((wl, wr)):
                link(v.tensor_tensor(attn_b[i], attn_b[i], wgat_sb[:, :, :].rearrange("p l d -> p (l d)"), ALU.mult))
                ins = v.tensor_reduce(o[:, :, :].rearrange("p l h -> p (l h)"),
                                      attn_b[i].rearrange("p (g j) -> p g j", j=DH), AX, ALU.add)
                link(ins)

            wide = dve.alloc_register("wide")
            rounds = dve.value_load(rounds_i[0:1, 0:1], min_val=1, max_val=NR)

            for n, name in enumerate(("part_kept", "sum_kept", "part_ready", "weights_set", "pair_kept", "er_kept")):
                v.memset(small[0:1, 120 + n:121 + n], 0.0).then_inc(S(name), 2 if name == "er_kept" else 1)

            def add_part(n3, addr, name, base, done):
                lk = linker(name, base)
                for i in range(NP):
                    a = acc[:, 0:n3, bass.ds(addr[i], W)]
                    ins = v.tensor_tensor(a, a, part[:, 0:n3, i * W:(i + 1) * W], ALU.add)
                    if i < NP - 1:
                        lk(ins)
                ins.then_inc(S(done), 1)

            cur = [dve.alloc_register(f"base{i}") for i in range(NP)]
            prev = [dve.alloc_register(f"prev{i}") for i in range(NP)]

            def values(regs):
                return [dve.snap(r_, min_val=0, max_val=N) for r_ in regs]

            def start_round(name, j, keyed):
                nk = 7 if keyed else 3
                lk = linker(name, j * (nk + 1))
                if keyed:
                    dve.wait_ge(S("weights_set"), j * PASSES + 1)
                lk(v.tensor_scalar(base_f, gbase[:, :], float(N), None, ALU.min))
                lk(v.tensor_copy(base_i[:, :, 0:NP], base_f.rearrange("p (s a) -> p s a", a=NP)))
                lk(v.tensor_tensor(ld[:, :].rearrange("p (a b) -> p a b", b=KT),
                                   dst_t[:, :].rearrange("p (a b) -> p a b", b=KT),
                                   spread(gbase[:, :], 2, KT), ALU.subtract))
                if keyed:
                    lk(v.tensor_scalar(relkey[:, :], ld[:, :], -(W - 1) / 2.0, None, ALU.add))
                    lk(v.tensor_tensor(relkey[:, :], relkey[:, :], relkey[:, :], ALU.mult))
                    lk(v.tensor_scalar(relkey[:, :], relkey[:, :], (W / 2.0) ** 2, 1.0e5, ALU.is_gt, ALU.mult))
                    lk(v.tensor_tensor(relkey[:, :], relkey[:, :], ld[:, :], ALU.add))
                    v.tensor_tensor(relkey[:, :], relkey[:, :], ety_t[:, :], ALU.add)
                dve.nop(nofuse=True)

            def end_round(name, j, keyed):
                nk = 7 if keyed else 3
                v.tensor_scalar(gbase[:, :], gbase[:, :], float(W), None, ALU.add).then_inc(S(name), 1)
                dve.wait_ge(S(name), j * (nk + 1) + (nk + 1))
                dve.nop(nofuse=True)

            def find_most(l):
                lk = linker(f"most_start{l}")
                lk(v.tensor_reduce(head_of, ident[0:HC, 0:HC].rearrange("p (h w) -> p h w", w=W), AX, ALU.add))
                lk(v.tensor_reduce(win_of, ident[0:HC, 0:HC].rearrange("p (h w) -> p w h", w=W), AX, ALU.add))
                v.memset(mwin_f[0:1, 0, 0:1], 0.0).then_inc(S(f"most_cols{l}"), 1)
                lk(v.memset(most_el, -FAR))
                lk(v.tensor_copy(gbase[:, :], gmin0[:, :]))
                with dve.Fori(0, rounds) as j:
                    start_round(f"most_round{l}", j, False)
                    with dve.Fori(0, SUPERS) as sp_no:
                        ql = dve.snap(j * SUPERS + sp_no)
                        dve.wait_ge(S(f"most_restarted{l}"), j + 1)
                        dve.nop(nofuse=True)
                        dve.load(cur, base_i[0:1, bass.ds(sp_no, 1), 0:NP])
                        bases = values(cur)
                        lk = linker(f"most_steps{l}", ql * (2 + 2 * NP))
                        lk(v.tensor_tensor(far[:, :, :], spread(iota[0:P, 0:W], 1, TS),
                                           spread(ld[:, bass.ds(sp_no * TS, TS)], 2, W), ALU.not_equal))
                        lk(v.tensor_scalar(far[:, :, :], far[:, :, :], -FAR, None, ALU.mult))
                        for i in range(NP):
                            n = dve.snap(ql * NP + i)
                            dve.wait_ge(gathered[0], (sp_no * NP + (i + 1)) * (16 * KT))
                            lk(v.tensor_tensor(raw, spread(far[:, i * KT:(i + 1) * KT, :], 2, H),
                                               spread(rows[:, 0:KT, D:D + H], 3, W), ALU.add))
                            v.tensor_reduce(mwin_f[:, 0, :], raw_f.rearrange("p t c -> p c t"), AX, ALU.max
                                            ).then_inc(S(f"most_cols{l}"), 1)
                            dve.wait_ge(S(f"most_turned{l}"), n + 1)
                            lk(v.tensor_reduce(most_col, bank[7][0:HC, 0:P], AX, ALU.max))
                            v.tensor_scalar(most_rhs, win_of, most_col, None, ALU.mult
                                            ).then_inc(S(f"most_spread{l}"), 1)
                            dve.wait_ge(S(f"most_heads{l}"), n + 1)
                            a = acc[0:H, 0, bass.ds(bases[i], W)]
                            v.tensor_tensor(a, a, bank[6][0:H, 0:W], ALU.max).then_inc(S(f"most_kept{l}"), 1)
                            dve.wait_ge(S(f"most_kept{l}"), n + 1)
                        dve.nop(nofuse=True)
                    end_round(f"most_round{l}", j, False)
                v.tensor_scalar(most_el, most_el, NONE, None, ALU.max).then_inc(S(f"most_ready{l}"), 1)
                dve.wait_ge(S(f"most_saved{l}"), 16)
                dve.wait_ge(S(f"most_restarted{l}"), rounds + 1)
                v.memset(small[0:1, 131:132], 0.0).then_inc(S(f"window_used{l}"), 1)
                lk = linker(f"most_end{l}")
                lk(v.memset(most_el, 0.0))

            def sweep(stage_no, exact):
                if stage_no:
                    dve.wait_ge(S("er_kept"), CHUNKS * H * stage_no + 2)
                    dve.nop(nofuse=True)
                l = stage_no - 1
                lk = linker("sweep_start", stage_no)
                lk(v.tensor_copy(gbase[:, :], gmin0[:, :]))
                with dve.Fori(0, rounds) as j:
                    jl = dve.snap(rounds * l + j) if stage_no else j
                    start_round("rounds_layer" if stage_no else "rounds_first", jl, stage_no > 0)
                    if exact:
                        v.memset(small[0:1, 130:131], 0.0).then_inc(S(f"bases_set{l}"), 1)
                    dve.wait_ge(S("restarted"), j + (1 if stage_no == 0 else rounds * stage_no + 1))
                    dve.nop(nofuse=True)
                    with dve.Fori(0, SUPERS) as sp_no:
                        q = dve.snap((rounds * stage_no + j) * SUPERS + sp_no)
                        ql = dve.snap(j * SUPERS + sp_no)
                        dve.load(cur, base_i[0:1, bass.ds(sp_no, 1), 0:NP])
                        bases = values(cur)
                        ld_s = spread(ld[:, bass.ds(sp_no * TS, TS)], 2, W)
                        cols_w = spread(iota[0:P, 0:W], 1, TS)
                        if stage_no == 0:
                            dve.wait_ge(S("passes_done"), (q + 1) * NP)
                            v.tensor_tensor(far[:, :, :], cols_w, ld_s, ALU.is_equal
                                            ).then_inc(S("hits_set"), 1)
                            dve.wait_ge(S("sum_ready"), q + 1)
                            add_part(1, bases, "added0", ql * (NP - 1), "sum_kept")
                        else:
                            qa = dve.snap((rounds * l + j) * SUPERS + sp_no)
                            lk = linker("far_steps", qa * 2)
                            lk(v.tensor_tensor(far[:, :, :], cols_w, ld_s, ALU.not_equal))
                            lk(v.tensor_scalar(far[:, :, :], far[:, :, :], -FAR, None, ALU.mult))
                            for i in range(NP):
                                g0 = i * KT
                                lk = linker("score_steps", (qa * NP + i) * 3)
                                er_w = er_b[0:P, :, bass.ds(bases[i], W)]
                                dve.wait_ge(gathered[i], (sp_no + 1) * (16 * KT))
                                v.tensor_tensor(raw, spread(far[:, g0:g0 + KT, :], 2, H),
                                                spread(rows[:, g0:g0 + KT, D:D + H], 3, W), ALU.add)
                                most = mwin[:, 0, :, :] if exact else spread(gmx[:, :], 2, W)
                                if exact:
                                    dve.wait_ge(S(f"window_loaded{l}"), ((ql * NP) + (i + 1)) * 16)
                                lk(v.tensor_tensor(mwin[:, 0, :, :], er_w, most, ALU.add))
                                v.tensor_tensor(raw, raw, spread(er_w, 1, KT), ALU.add)
                                lk(v.scalar_tensor_tensor(out=mwin[:, 1, :, :], in0=mwin[:, 0, :, :], scalar=SLOPE,
                                                          in1=mwin[:, 0, :, :], op0=ALU.mult, op1=ALU.max))
                                if exact:
                                    v.memset(small[0:1, 131:132], 0.0).then_inc(S(f"window_used{l}"), 1)
                                dve.wait_ge(S("weights_set"), qa * NP + (i + 1))
                                lk(v.scalar_tensor_tensor(out=score_f, in0=raw_f, scalar=SLOPE, in1=raw_f,
                                                          op0=ALU.mult, op1=ALU.max))
                                v.tensor_tensor(score_f, score_f,
                                                spread(mwin[:, 1, :, :].rearrange("p h w -> p (h w)"), 1, KT),
                                                ALU.subtract).then_inc(S("scores_set"), 1)
                                dve.wait_ge(S("passes_done"), q * NP + (4, 5, 5, 6, 7)[i])
                                for t in range(KT):
                                    ins = v.tensor_scalar(rel[:, RING[i], t, :], iota16[:, :],
                                                          relkey[:, bass.ds(sp_no * TS + (g0 + t), 1)], None,
                                                          ALU.is_equal)
                                ins.then_inc(S("onehots"), 1)
                                if i == 2:
                                    addr = values(prev)
                                    dve.wait_ge(S("part_ready"), qa + (stage_no + 1))
                                    add_part(3, addr, "added", qa * (NP - 1), "part_kept")
                            for a, b in zip(prev, bases):
                                dve.reg_mov(a, b)
                    end_round("rounds_layer" if stage_no else "rounds_first", jl, stage_no > 0)

            for stage_no in range(L + 1):
                l = stage_no - 1
                if stage_no:
                    lk = linker("largest_el", (stage_no - 1) * 6)
                    dve.wait_ge(S("el_kept"), CHUNKS * stage_no)
                    els = el_all[:, 0:N // P, :].rearrange("p n h -> p h n")
                    v.tensor_reduce(small[0:P, 0:H], els, AX, ALU.max)
                    lk(v.tensor_reduce(small[0:P, 8:8 + H], els, AX, ALU.min))
                    v.tensor_scalar(small[0:P, H:2 * H], small[0:P, 8:8 + H], -1.0, None, ALU.mult
                                    ).then_inc(S("el_max"), 1)
                    v.memset(agg_flat[:, :], 0.0).then_inc(S("zeros_set"), 1)
                    dve.wait_ge(S("el_max_t"), stage_no)
                    lk(v.tensor_reduce(small[0:2 * H, 16:17], bank[5][0:2 * H, 0:P], AX, ALU.max))
                    v.tensor_scalar(small[0:2 * H, 20:20 + 2 * H], ident[0:2 * H, 0:2 * H], small[0:2 * H, 16:17],
                                    None, ALU.mult).then_inc(S("el_diag"), 1)
                    dve.wait_ge(S("el_max_b"), stage_no)
                    lk(v.tensor_copy(gmx[:, :], bank[6][0:P, 0:H]))
                    lk(v.tensor_tensor(small[0:P, 30:30 + H], gmx[:, :], bank[6][0:P, H:2 * H], ALU.add))
                    lk(v.tensor_reduce(small[0:P, 35:36], small[0:P, 30:30 + H], AX, ALU.max))
                    v.tensor_scalar(el_wide[0:P, :], small[0:P, 35:36], WIDE, None, ALU.is_gt
                                    ).then_inc(S("el_wide_set"), 1)
                    v.memset(acc[:, 0:2, :], 0.0)
                    lk(v.memset(acc[:, 2, :], EMPTY))
                    dve.wait_ge(S("el_wide_set"), stage_no)
                    dve.nop(nofuse=True)
                    for r_ in prev:
                        dve.reg_mov(r_, 0)
                    dve.load(wide, el_wide[0:1, :])
                    with dve.If_eq(wide, 1):
                        find_most(l)
                if stage_no:
                    with dve.If_eq(wide, 1):
                        sweep(stage_no, True)
                    with dve.Else():
                        sweep(stage_no, False)
                else:
                    sweep(0, False)
                if stage_no:
                    qe = dve.snap(rounds * (SUPERS * stage_no))
                    addr = values(prev)
                    dve.wait_ge(S("part_ready"), qe + (stage_no + 1))
                    add_part(3, addr, "added_last", l * (NP - 1), "part_kept")
                lr = min(stage_no, L - 1)
                v.tensor_copy(row_w[:, D:SPLIT], wl[:, lr, :])
                v.tensor_copy(wr_b[:, :, :], spread(wr[:, lr, :], 2, P)).then_inc(S("sums_ready"), 1)
                def squares_sum(c, n):
                    dve.wait_ge(S("squared"), n + 1)
                    v.tensor_reduce(var[:, 0, bass.ds(c * CT, CT)],
                                    squares[:, bass.ds(c * CH2, CH2)].rearrange("p (k d) -> p k d", d=D),
                                    AX, ALU.add).then_inc(S("var_set"), 1)

                def deviation(n):
                    v.tensor_scalar(var[:, 1, :], var[:, 0, :], 1.0 / D, None, ALU.mult).then_inc(S("var_mean"), 1)
                    dve.wait_ge(S("deviation"), n + 1)
                    v.reciprocal(var[:, 2, :], var[:, 2, :]).then_inc(S("var_inverse"), 1)
                    dve.wait_ge(S("var_inverse"), n + 1)

                per_node = lambda k, a=0, b=N // P: spread(var[:, k, a:b], 2, D)
                if stage_no == 0:
                    with dve.Fori(0, CHUNKS) as c:
                        squares_sum(c, c)
                    dve.wait_ge(S("var_set"), CHUNKS)
                    deviation(0)
                    dve.wait_ge(S("pair_kept"), CHUNKS + 1)
                    lk = linker("residual_steps")
                    lk(v.tensor_tensor(normed_rows, normed_rows, per_node(2), ALU.mult))
                    lk(v.tensor_tensor(normed_rows, normed_rows, x_rows, ALU.add))
                    lk(v.tensor_reduce(var[:, 0, 0:N // P], normed_rows, AX, ALU.add))
                    lk(v.tensor_scalar(var[:, 1, :], var[:, 0, :], 1.0 / D, None, ALU.mult))
                    v.tensor_tensor(normed_rows, normed_rows, per_node(1), ALU.subtract).then_inc(S("x1_centred"), 1)
                    dve.wait_ge(S("x1_squared"), 1)
                    lk(v.tensor_reduce(var[:, 0, 0:N // P], squares_rows, AX, ALU.add))
                    deviation(1)
                    v.tensor_tensor(normed_rows, normed_rows, per_node(2), ALU.mult).then_inc(S("x1_rows"), 1)
                else:
                    fb = l * CHUNKS
                    with dve.Fori(0, CHUNKS) as c:
                        cc = bass.ds(c * CH, CH)
                        v.reciprocal(acc[:, 2, cc], acc[:, 2, cc]).then_inc(S("den_inverse"), 1)
                        dve.wait_ge(S("den_inverse"), c + (fb + 1))
                        v.tensor_tensor(acc[:, 1, cc], acc[:, 1, cc], acc[:, 2, cc], ALU.mult
                                        ).then_inc(S("branches"), 1)
                if stage_no < L:
                    k0 = stage_no * CHUNKS
                    for first, end in ((0, SLOTS), (SLOTS, CHUNKS)):
                        with dve.Fori(first, end) as c:
                            slot = dve.snap((c - first) * CT)
                            full = rows[:, bass.ds(slot, CT), 0:D]
                            piece = [rows_b[:, bass.ds(slot, CT), 2 * SPLIT + k * D:2 * SPLIT + (k + 1) * D]
                                     for k in range(PARTS)]
                            lk = linker("piece_steps", (c + k0) * 3)
                            dve.wait_ge(S("pair_kept"), c + (k0 + PAIRS0 + 2))
                            lk(v.tensor_copy(piece[0], full))
                            v.tensor_copy(el_all[:, bass.ds(c * CT, CT), :], rows[:, bass.ds(slot, CT), D:SPLIT]
                                          ).then_inc(S("el_kept"), 1)
                            lk(v.tensor_tensor(rest, full, piece[0], ALU.subtract))
                            lk(v.tensor_copy(piece[1], rest))
                            v.tensor_tensor(piece[2], rest, piece[1], ALU.subtract).then_inc(S("table_rows"), 1)
                else:
                    with dve.Fori(0, CHUNKS) as c:
                        squares_sum(c, c + CHUNKS)
                    dve.wait_ge(S("var_set"), 2 * CHUNKS)
                    deviation(2)
                    for a, b in OUT_PARTS:
                        v.tensor_tensor(normed_rows[:, a:b, :], normed_rows[:, a:b, :], per_node(2, a, b), ALU.mult
                                        ).then_inc(S("out_rows"), 1)

        @block.scalar
        def _(act):
            a_ = nc.scalar
            act.wait_ge(S("rounds_set"), 1)
            rounds = act.value_load(rounds_i[0:1, 0:1], min_val=1, max_val=NR)
            act.wait_ge(S("passes_done"), NP)
            act.wait_ge(S("folded"), 1)

            def centred_kept(c, part_no):
                a_.activation(squares[:, bass.ds(c * CH2, CH2)].rearrange("p (k d) -> p k d", d=D),
                              pair[:, :, 0:D], ACT.Square).then_inc(S("squared"), 1)
                a_.activation(normed[:, bass.ds(c * CH2, CH2)].rearrange("p (k d) -> p k d", d=D),
                              pair[:, :, part_no * D:(part_no + 1) * D], ACT.Copy).then_inc(S("pair_kept"), 1)

            def deviation(n):
                act.wait_ge(S("var_mean"), n + 1)
                a_.activation(var[:, 2, :], var[:, 1, :], ACT.Sqrt, bias=eps[0:P, 0:1]).then_inc(S("deviation"), 1)

            def keep_agg(i, q):
                act.wait_ge(S("passes_done"), q * NP + (i + (NP + 1)))
                a_.activation(agg[:, i, :], bank[RING[i]][:, 0:RC + HC], ACT.Copy).then_inc(S("agg_kept"), 1)

            def keep_den(qa, stage_no):
                act.wait_ge(S("part_kept"), qa + stage_no)
                for h in range(H):
                    den = bank[3][h * DH:(h + 1) * DH, 0:NP * HC].rearrange("p (i g w) -> p i g w", g=H, w=W)
                    ins = a_.activation(part[h * DH:(h + 1) * DH, 2, :].rearrange("p (i w) -> p i w", w=W),
                                        den[:, :, h, :], ACT.Copy)
                ins.then_inc(S("den_kept"), 1)

            def keep_part(qa, stage_no):
                act.wait_ge(S("projected"), qa + stage_no)
                a_.activation(part[:, 0, :], bank[4][:, 0:NP * W], ACT.Copy)
                a_.activation(part[:, 1, :], bank[5][:, 0:NP * W], ACT.Copy).then_inc(S("part_ready"), 1)

            for stage_no in range(L + 1):
                if stage_no:
                    with act.Fori(0, CHUNKS) as c:
                        for h in range(H):
                            act.wait_ge(S("er_major"), (c + (stage_no - 1) * CHUNKS) * H + (h + 1))
                            a_.activation(er_b[0:P, h, bass.ds(c * CH, CH)], bank[6 + h % 2][0:P, 0:CH], ACT.Copy
                                          ).then_inc(S("er_kept"), 1)
                    a_.activation(small[:, 150:151], eps[:, 0:1], ACT.Exp)
                    act.wait_ge(S("banks_zeroed"), stage_no)
                with act.Fori(0, rounds) as j:
                    with act.Fori(0, SUPERS) as sp_no:
                        q = act.snap((rounds * stage_no + j) * SUPERS + sp_no)
                        if stage_no == 0:
                            act.wait_ge(S("passes_done"), (q + 2) * NP)
                            a_.activation(part[:, 0, :], bank[0][:, 0:NP * W], ACT.Copy).then_inc(S("sum_ready"), 1)
                        else:
                            qa = act.snap((rounds * (stage_no - 1) + j) * SUPERS + sp_no)

                            def exponent(i):
                                act.wait_ge(S("scores_set"), qa * NP + (i + 1))
                                a_.activation(wts[:, RING[i], :, :], score_f, ACT.Exp
                                              ).then_inc(S("weights_set"), 1)

                            keep_agg(3, q - 1)
                            exponent(0)
                            keep_agg(4, q - 1)
                            keep_den(qa, stage_no)
                            exponent(1)
                            keep_part(qa, stage_no)
                            keep_agg(0, q)
                            exponent(2)
                            keep_agg(1, q)
                            exponent(3)
                            keep_agg(2, q)
                            exponent(4)
                if stage_no:
                    qe = act.snap(rounds * (SUPERS * stage_no))
                    q = act.snap(rounds * (SUPERS * (stage_no + 1)))
                    keep_agg(3, q - 1)
                    keep_agg(4, q - 1)
                    keep_den(qe, stage_no)
                    keep_part(qe, stage_no)

                if stage_no == 0:
                    act.wait_ge(S("sums_ready"), 1)
                    act.nop(nofuse=True)
                    with act.Fori(0, CHUNKS) as c:
                        a_.activation(hstage[:, :], acc[:, 0, bass.ds(c * CH, CH)], ACT.Copy
                                      ).then_inc(S("sums_staged"), 1)
                        act.wait_ge(S("sums_centred"), c + 1)
                        centred_kept(c, 1)
                    deviation(0)
                    act.wait_ge(S("x1_centred"), 1)
                    a_.activation(squares_rows, normed_rows, ACT.Square).then_inc(S("x1_squared"), 1)
                    deviation(1)
                    for c in range(CHUNKS):
                        act.wait_ge(S("x1_turned"), c + 1)
                        n = min(CH, N - c * CH)
                        a_.activation(h_t[:, c * CH:c * CH + n], bank[c % 2][:, 0:n], ACT.Copy
                                      ).then_inc(S("h_set"), 1)
                else:
                    l = stage_no - 1
                    if l == 0:
                        act.wait_ge(S("x1_saved"), 16)
                    with act.Fori(0, CHUNKS) as c:
                        cc = bass.ds(c * CH, CH)
                        act.wait_ge(S("fused"), c + (l * CHUNKS + 1))
                        if l == 0:
                            a_.activation(acc[:, 0, cc], bank[1][:, 0:CH], ACT.Identity,
                                          bias=cols[:, BREL + l:BREL + l + 1]).then_inc(S("gate_in"), 1)
                        ins = a_.activation(h_t[:, cc], bank[1][:, 0:CH], ACT.Relu, bias=cols[:, BREL + l:BREL + l + 1])
                        if l == 0:
                            act.wait_ge(S("gated"), c + 1)
                            ins = a_.activation(acc[:, 2, cc], bank[2][:, 0:CH], ACT.Sigmoid, bias=cols[:, GB:GB + 1])
                        ins.then_inc(S("h_set"), 1)
                k0 = stage_no * CHUNKS
                if stage_no < L:
                    for first, end in ((0, SLOTS), (SLOTS, CHUNKS)):
                        if first:
                            for c in range(first, end):
                                b = (c - first) % 2
                                act.wait_ge(table_written[b], 16 * (stage_no * WRITES[b] + (c - first) // 2 + 1))
                            act.nop(nofuse=True)
                        with act.Fori(first, end) as c:
                            act.wait_ge(S("rows_major"), c + (k0 + 2))
                            a_.activation(rows[:, bass.ds((c - first) * CT, CT), 0:SPLIT], pair[:, :, 0:SPLIT], ACT.Copy
                                          ).then_inc(S("pair_kept"), 1)
                else:
                    with act.Fori(0, CHUNKS) as c:
                        act.wait_ge(S("rows_major"), c + (k0 + 2))
                        centred_kept(c, 0)
                    deviation(2)


NAMES = ["x", "src", "dst", "edge_type_16", "edge_weight", "L0_gnn_W", "L0_gnn_b", "L0_gnn_gamma", "L0_gnn_beta",
         "L1_gnn_W_rel", "L1_gnn_b_rel", "L1_gnn_W_loop", "L1_gnn_W_gat", "L1_gnn_attn_l", "L1_gnn_attn_r",
         "L1_gnn_b_gat", "L1_gnn_W_fuse", "L1_gnn_b_fuse", "L1_gnn_W_gate", "L1_gnn_b_gate"]


def kernel(**inputs):
    import concourse.bacc as bacc
    from concourse.bass_utils import run_bass_kernel_spmd

    nc = bacc.Bacc("TRN2", target_bir_lowering=False, num_devices=1)
    arrays, args = {}, []
    for name in NAMES:
        a = np.ascontiguousarray(inputs[name])
        arrays[f"in_{name}"] = a
        args.append(nc.dram_tensor(f"in_{name}", a.shape, mybir.dt.from_np(a.dtype), kind="ExternalInput").ap())
    out = nc.dram_tensor("out_x", (N, D), F32, kind="ExternalOutput").ap()
    tables = [nc.dram_tensor(f"table{l}", (NPAD, ROW), F32, kind="Internal").ap() for l in range(L)]
    x1_dram = nc.dram_tensor("x1_t", (D, NPAD), F32, kind="Internal").ap()
    most_dram = nc.dram_tensor("most_el", (H, NPAD), F32, kind="Internal").ap()
    build(nc, *args, out, tables, x1_dram, most_dram)
    return run_bass_kernel_spmd(nc, [arrays], core_ids=[0]).results[0]["out_x"]
```
